# Optimizing a Trainium2 kernel written in Bass

```python
import numpy as np
import jax
import jax.numpy as jnp

def _softmax(x, axis=-1):
    return jax.nn.softmax(x, axis=axis)

def _gelu(x):
    return jax.nn.gelu(x, approximate=True)

def _silu(x):
    return jax.nn.silu(x)

def _sigmoid(x):
    return jax.nn.sigmoid(x)

def _layernorm(x, axis=-1, eps=1e-05):
    m = jnp.mean(x, axis=axis, keepdims=True)
    v = jnp.var(x, axis=axis, keepdims=True)
    return (x - m) / jnp.sqrt(v + eps)

def _scatter_add(tgt, idx, src, axis=0):
    return tgt.at[idx].add(src)

def _segment_sum(src, seg, n):
    return jax.ops.segment_sum(src, seg, n)
kernel_name = 'mk_prb_d1_jaxref_r4_2d4126'

def setup_inputs(seed: int=0):
    np.random.seed(seed)
    _w = jnp.asarray

    def _L0_attn_setup():
        import jax, jax.numpy as jnp
        import numpy as np
        EMBED_DIM = 256
        NUM_HEADS = 16
        HEAD_DIM = EMBED_DIM // NUM_HEADS
        SEQ_LEN = 256
        BATCH = 4
        MAX_REL_POS = 2

        def _rel_index(length_q, length_k):
            q = jnp.arange(length_q)[:, None]
            k = jnp.arange(length_k)[None, :]
            return jnp.clip(k - q, -MAX_REL_POS, MAX_REL_POS) + MAX_REL_POS
        key = jax.random.key(seed)
        ks = jax.random.split(key, 12)
        s = 1.0 / np.sqrt(EMBED_DIM)
        x = jax.random.normal(ks[0], (BATCH, SEQ_LEN, EMBED_DIM), dtype=jnp.float32)
        W_q = jax.random.normal(ks[1], (EMBED_DIM, EMBED_DIM), dtype=jnp.float32) * s
        b_q = jnp.zeros((EMBED_DIM,), dtype=jnp.float32)
        W_k = jax.random.normal(ks[2], (EMBED_DIM, EMBED_DIM), dtype=jnp.float32) * s
        b_k = jnp.zeros((EMBED_DIM,), dtype=jnp.float32)
        W_v = jax.random.normal(ks[3], (EMBED_DIM, EMBED_DIM), dtype=jnp.float32) * s
        b_v = jnp.zeros((EMBED_DIM,), dtype=jnp.float32)
        W_o = jax.random.normal(ks[4], (EMBED_DIM, EMBED_DIM), dtype=jnp.float32) * s
        b_o = jnp.zeros((EMBED_DIM,), dtype=jnp.float32)
        lim = float(np.sqrt(6.0 / (2 * MAX_REL_POS + 1 + HEAD_DIM)))
        rel_k_table = jax.random.uniform(ks[5], (2 * MAX_REL_POS + 1, HEAD_DIM), jnp.float32, -lim, lim)
        rel_v_table = jax.random.uniform(ks[6], (2 * MAX_REL_POS + 1, HEAD_DIM), jnp.float32, -lim, lim)
        return {'x': x, 'W_q': W_q, 'b_q': b_q, 'W_k': W_k, 'b_k': b_k, 'W_v': W_v, 'b_v': b_v, 'W_o': W_o, 'b_o': b_o, 'rel_k_table': rel_k_table, 'rel_v_table': rel_v_table}
    _L0_attn_in = _L0_attn_setup()

    def _L0_ffn_setup():
        import jax, jax.numpy as jnp
        import numpy as np
        DIM = 256

        def _reference_tuple_inner(x, W_r, W_k, W_v, mu_r, mu_k):
            B, T, C = x.shape
            x_prev = jnp.concatenate([jnp.zeros((B, 1, C), x.dtype), x[:, :-1, :]], axis=1)
            xr = mu_r * x + (1.0 - mu_r) * x_prev
            xk = mu_k * x + (1.0 - mu_k) * x_prev
            r = jax.nn.sigmoid(jnp.einsum('btc,dc->btd', xr, W_r))
            k = jnp.einsum('btc,dc->btd', xk, W_k)
            k_act = jnp.square(jax.nn.relu(k))
            out = r * jnp.einsum('btc,dc->btd', k_act, W_v)
            new_state = x[:, -1, :]
            return (out, new_state)
        key = jax.random.key(seed)
        ks = jax.random.split(key, 6)
        B, T, C = (8, 512, DIM)
        x = jax.random.normal(ks[0], (B, T, C), dtype=jnp.float32)
        s = 1.0 / np.sqrt(C)
        W_r = jax.random.uniform(ks[1], (C, C), jnp.float32, -s, s)
        W_k = jax.random.uniform(ks[2], (C, C), jnp.float32, -s, s)
        W_v = jax.random.uniform(ks[3], (C, C), jnp.float32, -s, s)
        mu_r = jax.random.uniform(ks[4], (C,), jnp.float32)
        mu_k = jax.random.uniform(ks[5], (C,), jnp.float32)
        return {'x': x, 'W_r': W_r, 'W_k': W_k, 'W_v': W_v, 'mu_r': mu_r, 'mu_k': mu_k}
    _L0_ffn_in = _L0_ffn_setup()
    _d = {'L0_attn_x': _L0_attn_in['x'], 'L0_attn_W_q': _L0_attn_in['W_q'], 'L0_attn_b_q': _L0_attn_in['b_q'], 'L0_attn_W_k': _L0_attn_in['W_k'], 'L0_attn_b_k': _L0_attn_in['b_k'], 'L0_attn_W_v': _L0_attn_in['W_v'], 'L0_attn_b_v': _L0_attn_in['b_v'], 'L0_attn_W_o': _L0_attn_in['W_o'], 'L0_attn_b_o': _L0_attn_in['b_o'], 'L0_attn_rel_k_table': _L0_attn_in['rel_k_table'], 'L0_attn_rel_v_table': _L0_attn_in['rel_v_table'], 'L0_ffn_W_r': _L0_ffn_in['W_r'], 'L0_ffn_W_k': _L0_ffn_in['W_k'], 'L0_ffn_W_v': _L0_ffn_in['W_v'], 'L0_ffn_mu_r': _L0_ffn_in['mu_r'], 'L0_ffn_mu_k': _L0_ffn_in['mu_k']}
    _x0 = _d['L0_attn_x']
    _d['L0_attn_x'] = jax.random.normal(jax.random.fold_in(jax.random.key(seed), 1), (8, 512, 256), dtype=_x0.dtype)
    del _x0
    return _d

def reference(L0_attn_x, L0_attn_W_q, L0_attn_b_q, L0_attn_W_k, L0_attn_b_k, L0_attn_W_v, L0_attn_b_v, L0_attn_W_o, L0_attn_b_o, L0_attn_rel_k_table, L0_attn_rel_v_table, L0_ffn_W_r, L0_ffn_W_k, L0_ffn_W_v, L0_ffn_mu_r, L0_ffn_mu_k):

    def _L0_attn_ref(x, W_q, b_q, W_k, b_k, W_v, b_v, W_o, b_o, rel_k_table, rel_v_table):
        import jax, jax.numpy as jnp
        import numpy as np
        EMBED_DIM = 256
        NUM_HEADS = 16
        HEAD_DIM = EMBED_DIM // NUM_HEADS
        SEQ_LEN = 256
        BATCH = 4
        MAX_REL_POS = 2

        def _rel_index(length_q, length_k):
            q = jnp.arange(length_q)[:, None]
            k = jnp.arange(length_k)[None, :]
            return jnp.clip(k - q, -MAX_REL_POS, MAX_REL_POS) + MAX_REL_POS
        B, S, E = x.shape
        H, D = (NUM_HEADS, HEAD_DIM)
        scale = jnp.sqrt(jnp.asarray(D, x.dtype))
        Q = x @ W_q + b_q
        K = x @ W_k + b_k
        V = x @ W_v + b_v
        Qh = Q.reshape(B, S, H, D).transpose(0, 2, 1, 3)
        Kh = K.reshape(B, S, H, D).transpose(0, 2, 1, 3)
        Vh = V.reshape(B, S, H, D).transpose(0, 2, 1, 3)
        scores = jnp.einsum('bhqd,bhkd->bhqk', Qh, Kh)
        idx = _rel_index(S, S)
        rel_k = rel_k_table[idx]
        scores = (scores + jnp.einsum('bhqd,qkd->bhqk', Qh, rel_k)) / scale
        causal = jnp.tril(jnp.ones((S, S), dtype=bool))
        scores = jnp.where(causal[None, None], scores, jnp.asarray(-1000000000.0, scores.dtype))
        attn = jax.nn.softmax(scores, axis=-1)
        out = jnp.einsum('bhqk,bhkd->bhqd', attn, Vh)
        rel_v = rel_v_table[idx]
        out = out + jnp.einsum('bhqk,qkd->bhqd', attn, rel_v)
        out = out.transpose(0, 2, 1, 3).reshape(B, S, E)
        return out @ W_o + b_o

    def _L0_ffn_ref(x, W_r, W_k, W_v, mu_r, mu_k):
        import jax, jax.numpy as jnp
        import numpy as np
        DIM = 256

        def _reference_tuple_inner(x, W_r, W_k, W_v, mu_r, mu_k):
            B, T, C = x.shape
            x_prev = jnp.concatenate([jnp.zeros((B, 1, C), x.dtype), x[:, :-1, :]], axis=1)
            xr = mu_r * x + (1.0 - mu_r) * x_prev
            xk = mu_k * x + (1.0 - mu_k) * x_prev
            r = jax.nn.sigmoid(jnp.einsum('btc,dc->btd', xr, W_r))
            k = jnp.einsum('btc,dc->btd', xk, W_k)
            k_act = jnp.square(jax.nn.relu(k))
            out = r * jnp.einsum('btc,dc->btd', k_act, W_v)
            new_state = x[:, -1, :]
            return (out, new_state)
        return _reference_tuple_inner(x, W_r, W_k, W_v, mu_r, mu_k)[0]
    x = L0_attn_x
    xn = _layernorm(x, axis=-1)
    x = x + _L0_attn_ref(xn, L0_attn_W_q, L0_attn_b_q, L0_attn_W_k, L0_attn_b_k, L0_attn_W_v, L0_attn_b_v, L0_attn_W_o, L0_attn_b_o, L0_attn_rel_k_table, L0_attn_rel_v_table) + _L0_ffn_ref(xn, L0_ffn_W_r, L0_ffn_W_k, L0_ffn_W_v, L0_ffn_mu_r, L0_ffn_mu_k)
    return x

_drawn_inputs = setup_inputs


def setup_inputs(seed=0):
    import zlib

    import numpy as np

    out = dict(_drawn_inputs(seed))
    spreads = {'L0_attn_b_q': (0.0, 0.619),
     'L0_attn_b_k': (0.0, 0.8),
     'L0_attn_b_v': (0.0, 0.1),
     'L0_attn_b_o': (0.0, 0.1)}
    factors = {'L0_attn_rel_k_table': 2.915, 'L0_ffn_W_r': 3.439, 'L0_ffn_mu_r': 6.917}
    for name, (base, spread) in spreads.items():
        noise = np.random.default_rng([zlib.crc32(name.encode()), seed]).standard_normal(out[name].shape)
        drawn = base * np.exp(spread * noise) if base else spread * noise
        out[name] = jnp.asarray(drawn.astype(out[name].dtype))
    for name, factor in factors.items():
        out[name] = (out[name] * factor).astype(out[name].dtype)
    return out
```

```python
from contextlib import ExitStack

import concourse.bass as bass
from concourse import mybir

F32 = mybir.dt.float32
F16 = mybir.dt.float16
ALU = mybir.AluOpType
ACT = mybir.ActivationFunctionType

P = 128
HEADS, HD = 16, 16
CH = 2
GROUP = 4
STEPS = 8
SLOTS = 8
LEAD = 3
SCALE = 0.25
M_UNIT = 64.0
MASKED = -1e30
EPS = 1e-5
ROOT_GUESS = 0x5F3759DF
NEWTON = 3

KEY_AT = [768, 0, 512, 384]
KEY_STEP = 384
HEAD_COLS = 1280
FILLS = [
    (0, [(0, 0, 0)]),
    (1, [(0, 1, 0), (0, 3, 384)]),
    (2, [(1, 0, 0)]),
    (0, [(1, 1, 0), (1, 3, 384)]),
    (1, [(0, 2, 0), (1, 2, 256)]),
]
FILL_BACK = [2, 2, 5, 3, 3]
FILL_SLOT = {0: 0, 1: 1, 3: 2, 4: 3, 6: 4}

JOBS = [
    ("heads_taken", 0), ("ffn_v_taken", 0), ("xf_stored", 0), ("xf_stored", 1), ("q_taken", 0),
    ("m_copied", 0), ("k_taken", 0), ("q_taken", 1), ("heads_taken", 1), ("k_taken", 1),
    ("band_taken", 0), ("m_copied", 1), ("band_taken", 1), ("yT_stored", 0), ("yT_stored", 1),
    ("v_stored", 0), ("heads_taken", 2), ("summed", 0), ("summed", 1), ("m_copied", 2),
    ("v_stored", 1), ("ffn_k_taken", 0), ("heads_taken", 3), ("ffn_k_taken", 1), ("gate_taken", 0),
    ("m_copied", 3), ("gate_taken", 1), ("ffn_v_taken", 1),
]


class Batch:

    def __init__(self, offset, register=None):
        self.offset, self.register = offset, register

    def __add__(self, n):
        return Batch(self.offset + n, self.register)

    def __sub__(self, n):
        return self + -n

    @property
    def parity(self):
        return self.offset % 2

    def real(self, batches):
        return self.register is not None or 0 <= self.offset < batches

    def index(self):
        return self.offset if self.register is None else self.register * 2 + self.offset


class Count:

    def __init__(self, sem, n, first, unit=1):
        self.sem, self.n, self.first, self.unit = sem, n, first, unit

    def after(self, it, pos):
        fixed = (self.n * (it.offset - self.first[0]) + pos - self.first[1] + 1) * self.unit
        if it.register is None:
            return self.sem, max(fixed, 0)
        assert fixed > 0, "an event before the first, in the loop"
        return self.sem, it.register * (2 * self.n * self.unit) + fixed

    def happened(self, it, pos):
        return it.register is not None or (it.offset, pos) >= self.first


def rwkv_attention_block(nc, x, W_q, b_q, W_k, b_k, W_v, b_v, W_o, b_o, rel_k, rel_v, W_r, W_fk, W_fv,
                         mu_r, mu_k, out):
    BATCHES, SEQ, E = x.shape
    TB = SEQ // P
    NG = HEADS // GROUP
    assert E == CH * P and SEQ == 512 and HEADS * HD == E and BATCHES == 8

    x_rows = x.rearrange("b (t p) e -> b p t e", p=P)
    out_rows = out.rearrange("b (t p) e -> b p t e", p=P)

    with ExitStack() as ctx:
        def sb(name, shape, dt=F32):
            return ctx.enter_context(nc.sbuf_tensor(name, shape, dt))

        def sem(name):
            return ctx.enter_context(nc.semaphore(name))

        w_q, w_k, w_v, w_o = (sb(f"w_{n}", [P, CH, E]) for n in "qkvo")
        w_rT, w_fkT, w_fvT = (sb(n, [P, CH, E]) for n in ("w_rT", "w_fkT", "w_fvT"))
        rows = sb("rows", [1, 6, E])
        rel_row = sb("rel_row", [1, 3, HD])
        b_k_row = sb("b_k_row", [1, E])
        mu_rows = sb("mu_rows", [1, 2, E])
        cols = sb("cols", [P, 6, CH])
        rel_v_all = sb("rel_v_all", [P, 3, HD])
        b_v_all = sb("b_v_all", [P, E])
        b_o_all = sb("b_o_all", [P, E])
        v_bias = sb("v_bias", [P, 3, E])
        ident = sb("ident", [P, P])
        ident16 = sb("ident16", [P, P], F16)
        head_ones = sb("head_ones", [P, 8])
        one = sb("one", [1, 1])
        key_mask = sb("key_mask", [P, SEQ])
        x_nat = [sb(f"x_nat{i}", [P, TB, E]) for i in range(2)]
        w_sum = [sb(f"w_sum{i}", [P, TB, E]) for i in range(2)]
        stats = sb("stats", [P, TB, 6])
        mean_var = sb("mean_var", [P, TB, 2])
        rstd, var_eps, root_a, root_b = (sb(n, [P, TB]) for n in ("rstd", "var_eps", "root_a", "root_b"))
        xn = sb("xn", [P, TB, E])
        xf = sb("xf", [P, CH, SEQ + 1])
        dx = sb("dx", [P, CH, SEQ])
        xr = sb("xr", [P, CH, SEQ])
        xk = dx
        qf = sb("qf", [P, CH, SEQ])
        qh, ql, kh, kl = (sb(n, [P, CH, SEQ], F16) for n in ("qh", "ql", "kh", "kl"))
        band_prod = sb("band_prod", [P, 2, CH, SEQ])
        band = [sb(f"band{i}", [P, TB, 2, HEADS]) for i in range(2)]
        v0 = [sb(f"v0_{i}", [P, TB, HEADS, 2 * HD]) for i in range(2)]
        v_own = [sb(f"v_own{i}", [P, TB, E]) for i in range(2)]
        v_prev = [sb(f"v_prev{i}", [P, TB, E]) for i in range(2)]
        v_next = sb("v_next", [P, TB, E])
        ffn_act = sb("ffn_act", [P, CH, SEQ])
        gate = sb("gate", [P, TB, E])
        q_stack = [sb(f"q_stack{g}", [P, GROUP, SEQ], F16) for g in range(NG)]
        k_stack = [sb(f"k_stack{g}", [P, GROUP, SEQ], F16) for g in range(NG)]
        probs = [sb(f"probs{i}", [P, GROUP, HEAD_COLS]) for i in range(2)]
        spill = [sb(f"spill{i}", [P, SEQ], F16) for i in range(2)]
        mx = [sb(f"mx{g}", [P, GROUP, TB]) for g in range(NG)]
        m_own = sb("m_own", [P, GROUP, TB])
        m_all = sb("m_all", [P, GROUP, TB])
        m16 = [sb(f"m16_{g}", [P, GROUP, TB], F16) for g in range(NG)]
        mT = sb("mT", [HEADS, P], F16)
        band_arg = [sb(f"band_arg{g}", [P, 2, GROUP, TB]) for g in range(NG)]
        band_exp = [sb(f"band_exp{g}", [P, 2, GROUP, TB]) for g in range(NG)]
        band_sum = sb("band_sum", [P, GROUP, TB])
        band_a = sb("band_a", [P, TB, GROUP, HD])
        band_b = sb("band_b", [P, TB, GROUP, HD])
        band_v = sb("band_v", [P, TB, GROUP, HD])
        oT = sb("oT", [P, SEQ])
        denom = sb("denom", [P, TB, GROUP])
        inv = sb("inv", [P, TB, GROUP])
        num = sb("num", [P, TB, GROUP, HD])
        y = sb("y", [P, TB, E])
        yT = sb("yT", [P, CH, SEQ])

        split_q = [nc.dram_tensor(f"split_q{c}", (2 * P, SEQ), F16, kind="Internal").ap() for c in range(CH)]
        split_k = [nc.dram_tensor(f"split_k{c}", (2 * P, SEQ), F16, kind="Internal").ap() for c in range(CH)]

        bank = [ctx.enter_context(nc.psum_tensor(f"bank{i}", [P, 512], F32)) for i in range(8)]
        max_bank, fill_bank, o_bank, spare = bank[0:2], bank[2:5], bank[5], bank[6:8]

        weights_in, rows_in = sem("weights_in"), sem("rows_in")
        consts_ready, vconsts_ready, turned_weights, cols_made = (
            sem(n) for n in ("consts_ready", "vconsts_ready", "turned_weights", "cols_made"))
        setup_taken, rows_ready = sem("setup_taken"), sem("rows_ready")

        pool_waited, dve_waited, sp_waited = sem("pool_waited"), sem("dve_waited"), sem("sp_waited")

        def count(name, n, first, unit=1):
            return Count(sem(name), n, first, unit)

        x_loaded = count("x_loaded", 1, (-2, 0), 16)
        ln_step = count("ln_step", 2, (-2, 0))
        root_step = count("root_step", 3 * NEWTON + 2, (-2, 0))
        xn_made = count("xn_made", 1, (-2, 0))
        xn_turned = count("xn_turned", 2, (-1, 0))
        xf_stored = count("xf_stored", 2, (-1, 0))
        q_made = count("q_made", 2, (-1, 0))
        q_taken = count("q_taken", 2, (-1, 0))
        q_low = count("q_low", 2, (-1, 0))
        k_made = count("k_made", 2, (-1, 0))
        k_high = count("k_high", 2, (-1, 0))
        k_low = count("k_low", 2, (-1, 0))
        k_taken = count("k_taken", 2, (-1, 0))
        split_stored = [count(f"split_stored{c}", 4, (-1, 0), 16) for c in range(CH)]
        stack_loaded = [count(f"stack_loaded{g}", 6, (0 if g == 3 else -1, 0), 16) for g in range(NG)]
        band_summed = count("band_summed", 2, (-1, 0))
        band_taken = count("band_taken", 2, (-1, 0))
        v_made = count("v_made", 2, (-1, 0))
        v_stored = count("v_stored", 2, (-1, 0))
        v_shifted = count("v_shifted", 3, (-1, 0), 16)
        dx_made = count("dx_made", 2, (-1, 0))
        mixed = count("mixed", 4, (-1, 0))
        ffn_k_made = count("ffn_k_made", 2, (-1, 0))
        relu_made = count("relu_made", 2, (-1, 0))
        ffn_k_taken = count("ffn_k_taken", 2, (-1, 0))
        gate_made = count("gate_made", 2, (-1, 0))
        gate_taken = count("gate_taken", 2, (-1, 0))
        gate_ready = count("gate_ready", 2, (-1, 0))
        ffn_v_made = count("ffn_v_made", 2, (-1, 1))
        ffn_v_taken = count("ffn_v_taken", 2, (-1, 1))
        ffn_added = count("ffn_added", 2, (-1, 1))
        residual_copied = count("residual_copied", 2, (-1, 0))
        max_scored = count("max_scored", 64, (-1, 40))
        max_taken = count("max_taken", 64, (-1, 40))
        m_step = count("m_step", 8, (-1, 6))
        m_rounded = count("m_rounded", 4, (-1, 3))
        band_shifted = count("band_shifted", 4, (-1, 3))
        band_exped = count("band_exped", 4, (-1, 3))
        m_turned = count("m_turned", 4, (-1, 3))
        m_copied = count("m_copied", 4, (-1, 3))
        m_row = [count(f"m_row{g}", 1, (-1 if g == 0 else 0, 0), 16) for g in range(NG)]
        scored = count("scored", 40, (0, 0))
        probs_made = count("probs_made", 40, (0, 0))
        diagonals_masked = count("diagonals_masked", 8, (0, 0))
        probs_masked = count("probs_masked", 8, (0, 0))
        o_added = count("o_added", 4, (0, 1))
        o_taken = count("o_taken", 4, (0, 2))
        band_step = count("band_step", 12, (0, 3))
        band_values = count("band_values", 4, (0, 1))
        heads_turned = count("heads_turned", 4, (0, 2))
        heads_taken = count("heads_taken", 4, (0, 2))
        head_step = count("head_step", 8, (0, 4))
        y_made = count("y_made", 4, (0, 2))
        y_turned = count("y_turned", 2, (1, 0))
        yT_stored = count("yT_stored", 2, (1, 0))
        o_made = count("o_made", 2, (1, 0))
        summed = count("summed", 2, (1, 0))
        out_stored = [count(f"out_stored{j}", 1, (1, 0), 16) for j in range(2)]

        by_name = dict(heads_taken=heads_taken, ffn_v_taken=ffn_v_taken, xf_stored=xf_stored,
                       q_taken=q_taken, m_copied=m_copied, k_taken=k_taken, band_taken=band_taken,
                       yT_stored=yT_stored, v_stored=v_stored, summed=summed, ffn_k_taken=ffn_k_taken,
                       gate_taken=gate_taken)

        def spare_free(job, it):
            n, at = job - 2, it
            while True:
                if n < 0:
                    n, at = n + len(JOBS), at - 1
                kind, pos = by_name[JOBS[n][0]], JOBS[n][1]
                if kind in (yT_stored, summed) or (kind is heads_taken and pos < 2):
                    of = at - 1
                elif kind is heads_taken or (kind is m_copied and pos < 3) or (kind is ffn_v_taken and pos == 0):
                    of = at
                else:
                    of = at + 1
                if at.offset < -1 or of.real(BATCHES):
                    return kind.after(at, pos)
                n -= 2

        def iterations(eng, body):
            for b in (-2, -1, 0):
                body(Batch(b))
            with eng.Fori(0, 3) as i:
                body(Batch(1, i))
                body(Batch(2, i))
            for b in (7, 8):
                body(Batch(b))

        def has_ln(it):
            return it.register is not None or it.offset <= 6

        def max_target(it, s):
            return (it, s + LEAD) if s + LEAD < STEPS else (it + 1, s + LEAD - STEPS)

        SETTLE = {1: (0, 1), 3: (0, 2), 5: (0, 3), 7: (1, 0)}
        TAIL = {0: (-1, 2), 2: (-1, 3), 4: (0, 0), 6: (0, 1)}
        BAND = {1: (-1, 3), 3: (0, 0), 5: (0, 1), 7: (0, 2)}

        block = ctx.enter_context(nc.Block())

        @block.sync
        def _(sp):
            for src, dst in ((W_q, w_q), (W_k, w_k), (W_v, w_v), (W_o, w_o)):
                sp.dma_start(dst[:, :, :], src.rearrange("(c p) n -> p c n", p=P)).then_inc(weights_in, 16)
            for n, src in enumerate((W_r, W_fk, W_fv)):
                sp.dma_start(probs[0][:, n, 0:CH * E].rearrange("p (c n) -> p c n", c=CH),
                             src.rearrange("(c p) n -> p c n", p=P)).then_inc(weights_in, 16)

            def load_stack(it, g):
                c, half = g // 2, g % 2
                q_src = split_q[c][half * P:(half + 1) * P, :]
                k_src = split_k[c][half * P:(half + 1) * P, :]
                sp.wait_ge(*split_stored[c].after(it, 3))
                sp.sem_inc(sp_waited, 1)
                if it.register is not None or it.offset >= 0:
                    sp.wait_ge(*scored.after(it, 10 * g + 9))
                both = "(h r) t -> r h t"
                sp.dma_start(q_stack[g][0:32, :, :], q_src.rearrange(both, r=32)).then_inc(stack_loaded[g].sem, 16)
                sp.dma_start(k_stack[g][0:32, :, :], k_src.rearrange(both, r=32)).then_inc(stack_loaded[g].sem, 16)
                sp.dma_start(k_stack[g][32:64, :, :], k_src.rearrange(both, r=32)).then_inc(stack_loaded[g].sem, 16)
                halves = q_src.rearrange("(h l e) t -> l e h t", l=2, e=HD)
                sp.dma_start(q_stack[g][32:48, :, :], halves[1]).then_inc(stack_loaded[g].sem, 16)
                sp.dma_start(q_stack[g][48:64, :, :], halves[0]).then_inc(stack_loaded[g].sem, 16)
                sp.dma_start(q_stack[g][64:65, :, :], k_stack[g][65:66, :, :]).then_inc(stack_loaded[g].sem, 16)

            def store_split(it, c):
                for n, (src, dst, half, ready) in enumerate((
                        (qh, split_q, 0, q_taken), (ql, split_q, 1, q_low),
                        (kh, split_k, 0, k_high), (kl, split_k, 1, k_low))):
                    if n == 0 and (it.register is not None or it.offset >= 0):
                        for g in (2 * c, 2 * c + 1):
                            sp.wait_ge(*stack_loaded[g].after(it if g == 3 else it - 1, 5))
                            sp.sem_inc(sp_waited, 1)
                    sp.wait_ge(*ready.after(it, c))
                    sp.dma_start(dst[c].rearrange("(h l e) t -> h l e t", l=2, e=HD)[:, half, :, :],
                                 src[:, c, :]).then_inc(split_stored[c].sem, 16)

            def body(it):
                nxt, late = it + 1, it - 1
                if it.real(BATCHES):
                    load_stack(late, 3)
                if has_ln(it):
                    if it.register is not None or it.offset > -2:
                        sp.wait_ge(*ln_step.after(late, 0))
                        sp.sem_inc(sp_waited, 1)
                    if it.register is not None or it.offset >= 0:
                        sp.wait_ge(*residual_copied.after(late, 1))
                    ahead = it + 2
                    where = ahead.offset if it.register is None else ahead.index() % BATCHES
                    sp.dma_start(x_nat[it.parity][:, :, :], x_rows[bass.ds(where, 1)].rearrange("o p t e -> p (o t) e")
                                 if it.register is not None else x_rows[where]).then_inc(x_loaded.sem, 16)
                if nxt.real(BATCHES):
                    store_split(it, 0)
                    load_stack(it, 0)
                    store_split(it, 1)
                    load_stack(it, 1)
                if late.real(BATCHES):
                    for j in range(2):
                        sp.wait_ge(*summed.after(it, j))
                        at = late.index()
                        dst = (out_rows[bass.ds(at, 1)].rearrange("o p t e -> p (o t) e")
                               if it.register is not None else out_rows[at])
                        sp.dma_start(dst[:, 2 * j:2 * j + 2, :], w_sum[late.parity][:, 2 * j:2 * j + 2, :]).then_inc(out_stored[j].sem, 16)
                if nxt.real(BATCHES):
                    sp.wait_ge(*v_stored.after(it, 1))
                    sp.sem_inc(sp_waited, 1)
                    sp.wait_ge(*band_values.after(it, 0))
                    prev = v_prev[nxt.parity]
                    sp.dma_start(prev[1:113, :, :], v_next[0:112, :, :]).then_inc(v_shifted.sem, 16)
                    sp.dma_start(prev[113:128, :, :], v_next[112:127, :, :]).then_inc(v_shifted.sem, 16)
                    sp.dma_start(prev[0:1, 1:TB, :], v_next[127:128, 0:TB - 1, :]).then_inc(v_shifted.sem, 16)
                    load_stack(it, 2)

            iterations(sp, body)
            for j in range(2):
                sp.wait_ge(*out_stored[j].after(Batch(BATCHES), 0))

        @block.gpsimd
        def _(pool):
            for part, src in ((rows[0:1, 0, :], b_q), (b_k_row[:, :], b_k), (mu_rows[0:1, 0, :], mu_r),
                              (mu_rows[0:1, 1, :], mu_k)):
                pool.dma_start(part, src.rearrange("(o n) -> o n", o=1)).then_inc(rows_in, 16)
            pool.dma_start(rel_row[:, :, :], rel_k[0:3, :].rearrange("(o r) d -> o r d", o=1)).then_inc(rows_in, 16)
            pool.dma_start(rel_v_all[:, :, :],
                           rel_v[0:3, :].rearrange("(o r) d -> o r d", o=1).to_broadcast([P, 3, HD])).then_inc(rows_in, 16)
            pool.dma_start(b_v_all[:, :], b_v.rearrange("(o n) -> o n", o=1).to_broadcast([P, E])).then_inc(rows_in, 16)
            pool.dma_start(b_o_all[:, :], b_o.rearrange("(o n) -> o n", o=1).to_broadcast([P, E])).then_inc(rows_in, 16)
            nc.gpsimd.memset(ident[:, :], 0.0).then_inc(consts_ready, 1)
            nc.gpsimd.memset(head_ones[:, :], 1.0).then_inc(consts_ready, 1)
            nc.gpsimd.memset(key_mask[:, :], 0.0).then_inc(consts_ready, 1)
            pool.wait_ge(consts_ready, 3)
            nc.gpsimd.affine_select(out=ident[:, :], in_=ident[:, :], compare_op=ALU.not_equal, fill=1.0,
                                    base=0, pattern=[[-1, P]], channel_multiplier=1).then_inc(consts_ready, 1)
            nc.gpsimd.affine_select(out=head_ones[:, :], in_=head_ones[:, :], compare_op=ALU.is_ge, fill=0.0,
                                    base=0, pattern=[[-HD, 8]], channel_multiplier=1).then_inc(consts_ready, 1)
            nc.gpsimd.affine_select(out=key_mask[:, :], in_=key_mask[:, :], compare_op=ALU.is_ge, fill=MASKED,
                                    base=SEQ - P - 2, pattern=[[-1, SEQ]], channel_multiplier=1).then_inc(consts_ready, 1)
            pool.wait_ge(consts_ready, 6)
            nc.gpsimd.affine_select(out=head_ones[:, :], in_=head_ones[:, :], compare_op=ALU.is_ge, fill=0.0,
                                    base=HD - 1, pattern=[[HD, 8]], channel_multiplier=-1).then_inc(consts_ready, 1)
            nc.gpsimd.tensor_copy(ident16[:, :], ident[:, :]).then_inc(consts_ready, 1)
            nc.gpsimd.memset(one[:, :], 1.0).then_inc(consts_ready, 1)
            nc.gpsimd.memset(xf[:, :, 0:1], 0.0).then_inc(consts_ready, 1)
            nc.gpsimd.memset(band_prod[:, 1, :, 0:1], 0.0).then_inc(consts_ready, 1)
            for i in range(2):
                nc.gpsimd.memset(v_prev[i][0:1, 0, :], 0.0).then_inc(consts_ready, 1)
                nc.gpsimd.memset(v0[i][:, :, :, HD:2 * HD], 1.0).then_inc(consts_ready, 1)

            def body(it):
                nxt = it + 1
                for s in range(STEPS):
                    if s == 0 and it.real(BATCHES):
                        pool.wait_ge(*ffn_v_taken.after(it, 0))
                        w = w_sum[it.parity][:, 2:4, :]
                        nc.gpsimd.tensor_tensor(w, w, gate[:, 2:4, :], ALU.add).then_inc(ffn_added.sem, 1)
                    if s == 1 and nxt.real(BATCHES):
                        for c in range(CH):
                            pool.wait_ge(*xf_stored.after(it, c))
                            if c == 0:
                                pool.wait_ge(*mixed.after(it - 1, 3))
                            nc.gpsimd.tensor_tensor(dx[:, c, :], xf[:, c, 0:SEQ], xf[:, c, 1:SEQ + 1],
                                                    ALU.subtract).then_inc(dx_made.sem, 1)
                    if s in (1, 2) and nxt.real(BATCHES):
                        c = s - 1
                        pool.wait_ge(*q_taken.after(it, c))
                        pool.wait_ge(*split_stored[c].after(it - 1, 3))
                        nc.gpsimd.tensor_tensor(ql[:, c, :], qf[:, c, :], qh[:, c, :],
                                                ALU.subtract).then_inc(q_low.sem, 1)
                    if s in BAND and (it + BAND[s][0]).real(BATCHES):
                        at, g = it + BAND[s][0], BAND[s][1]
                        pos = g + 1
                        e_own = band_exp[g][:, 0].rearrange("p h t -> p t h")
                        e_prev = band_exp[g][:, 1].rearrange("p h t -> p t h")
                        hs = slice(GROUP * g * HD, GROUP * (g + 1) * HD)
                        own = v_own[at.parity][:, :, hs].rearrange("p t (h d) -> p t h d", d=HD)
                        prev = v_prev[at.parity][:, :, hs].rearrange("p t (h d) -> p t h d", d=HD)
                        wide = [P, TB, GROUP, HD]
                        pool.wait_ge(*band_exped.after(at, g - 1))
                        pool.wait_ge(*v_stored.after(at - 1, 1))
                        pool.wait_ge(*v_shifted.after(at - 1, 2))
                        pool.wait_ge(*heads_taken.after(at, g + 1))
                        nc.gpsimd.tensor_tensor(band_sum[:, :, :], band_exp[g][:, 0], band_exp[g][:, 1],
                                                ALU.add).then_inc(band_step.sem, 1)
                        nc.gpsimd.tensor_tensor(band_a[:, :, :, :], own, e_own.unsqueeze(3).to_broadcast(wide),
                                                ALU.mult).then_inc(band_step.sem, 1)
                        nc.gpsimd.tensor_tensor(band_b[:, :, :, :], prev, e_prev.unsqueeze(3).to_broadcast(wide),
                                                ALU.mult).then_inc(band_step.sem, 1)
                        pool.wait_ge(*band_step.after(at, 3 * pos + 2))
                        nc.gpsimd.tensor_tensor(band_v[:, :, :, :], band_a[:, :, :, :], band_b[:, :, :, :],
                                                ALU.add).then_inc(band_values.sem, 1)
                    if s in (5, 6) and nxt.real(BATCHES):
                        j = s - 5
                        pool.wait_ge(*out_stored[j].after(it, 0))
                        pool.wait_ge(*x_loaded.after(it - 1, 0))
                        w = w_sum[nxt.parity][:, 2 * j:2 * j + 2, :]
                        nc.gpsimd.tensor_tensor(w, x_nat[nxt.parity][:, 2 * j:2 * j + 2, :],
                                                b_o_all[:, :].unsqueeze(1).to_broadcast([P, 2, E]),
                                                ALU.add).then_inc(residual_copied.sem, 1)
                    if s == 6 and has_ln(it):
                        pool.wait_ge(*ln_step.after(it, 1))
                        pool.wait_ge(*xn_turned.after(it, 1))
                        pool.sem_inc(pool_waited, 1)
                        for t in range(TB):
                            last = nc.gpsimd.tensor_scalar(xn[:, t, :], x_nat[it.parity][:, t, :],
                                                           mean_var[:, t, 0:1], rstd[:, t:t + 1],
                                                           ALU.subtract, ALU.mult)
                        last.then_inc(xn_made.sem, 1)
                    if s == 7 and nxt.real(BATCHES):
                        for j in range(2):
                            pool.wait_ge(*gate_taken.after(it, j))
                            pool.sem_inc(pool_waited, 1)
                            g2 = gate[:, 2 * j:2 * j + 2, :]
                            nc.gpsimd.tensor_scalar(g2, g2, 0.5, 0.5, ALU.mult, ALU.add).then_inc(gate_ready.sem, 1)
                    if it.real(BATCHES):
                        g, i0 = s // 2, 2 * (s % 2)
                        pool.wait_ge(*probs_made.after(it, 5 * s + 4))
                        pool.sem_inc(pool_waited, 1)
                        pr = probs[g % 2][:, i0:i0 + 2, :]
                        for h in range(2):
                            part = pr[:, h, 0:3 * KEY_STEP].rearrange("p (j w) -> p j w", w=KEY_STEP)[:, :, 0:P + 1]
                            last = nc.gpsimd.affine_select(out=part, in_=part, compare_op=ALU.is_ge, fill=0.0, base=-2,
                                                           pattern=[[0, 3], [1, P + 1]], channel_multiplier=-1)
                        last.then_inc(diagonals_masked.sem, 1)
                        pool.wait_ge(*diagonals_masked.after(it, s))
                        pool.sem_inc(pool_waited, 1)
                        part = pr[:, :, KEY_AT[2]:KEY_AT[2] + P + 1]
                        nc.gpsimd.affine_select(out=part, in_=part, compare_op=ALU.is_ge, fill=0.0, base=-2,
                                                pattern=[[0, 2], [1, P + 1]],
                                                channel_multiplier=-1).then_inc(probs_masked.sem, 1)
                    if s == 7 and nxt.real(BATCHES):
                        pool.wait_ge(*ffn_v_taken.after(it, 1))
                        w = w_sum[nxt.parity][:, 0:2, :]
                        nc.gpsimd.tensor_tensor(w, w, gate[:, 0:2, :], ALU.add).then_inc(ffn_added.sem, 1)

            iterations(pool, body)

        @block.scalar
        def _(act):
            for n, dst in enumerate((w_rT, w_fkT, w_fvT)):
                act.wait_ge(turned_weights, n + 1)
                nc.scalar.activation(dst[:, :, :], bank[2 + n][:, :].rearrange("p (c n) -> p c n", c=CH),
                                     ACT.Copy).then_inc(setup_taken, 1)
            act.wait_ge(cols_made, 1)
            nc.scalar.activation(cols[:, :, :], o_bank[:, 0:12].rearrange("p (a c) -> p a c", c=CH),
                                 ACT.Copy).then_inc(setup_taken, 1)
            act.wait_ge(setup_taken, 4)

            def body(it):
                nxt, late = it + 1, it - 1
                for s in range(STEPS):
                    for k in range(SLOTS):
                        if k == 0 and s in TAIL and (it + TAIL[s][0]).real(BATCHES):
                            at, g = it + TAIL[s][0], TAIL[s][1]
                            act.wait_ge(*o_added.after(at, g + 1))
                            act.wait_ge(*heads_turned.after(at, g + 1))
                            nc.scalar.activation(oT[:, :], o_bank[:, :], ACT.Copy).then_inc(o_taken.sem, 1)
                        if s == 0 and k in (4, 5) and nxt.real(BATCHES):
                            c = k - 4
                            act.wait_ge(*xn_turned.after(it, c))
                            act.wait_ge(*mixed.after(late, 3))
                            nc.scalar.activation(xf[:, c, 1:SEQ + 1], spare[c][:, :], ACT.Copy).then_inc(xf_stored.sem, 1)
                        if (s, k) in ((1, 0), (1, 6)) and nxt.real(BATCHES):
                            c = k // 6
                            act.wait_ge(*q_made.after(it, c))
                            act.wait_ge(*k_taken.after(late, c))
                            act.wait_ge(*split_stored[c].after(late, 3))
                            nc.scalar.activation(qf[:, c, :], spare[(4, 7)[c] % 2][:, :], ACT.Identity,
                                                 bias=cols[:, 0, c:c + 1])
                            nc.scalar.activation(qh[:, c, :], spare[(4, 7)[c] % 2][:, :], ACT.Identity,
                                                 bias=cols[:, 0, c:c + 1]).then_inc(q_taken.sem, 1)
                        if k == 4 and s in (1, 2) and nxt.real(BATCHES):
                            c = s - 1
                            act.wait_ge(*k_made.after(it, c))
                            act.wait_ge(*split_stored[c].after(late, 3))
                            nc.scalar.activation(kh[:, c, :], spare[(6, 9)[c] % 2][:, :], ACT.Identity,
                                                 bias=cols[:, 1, c:c + 1]).then_inc(k_high.sem, 1)
                        if (s, k) in ((2, 6), (3, 3)) and nxt.real(BATCHES):
                            c = s - 2
                            act.wait_ge(*band_summed.after(it, c))
                            nc.scalar.activation(band[nxt.parity][:, :, :, 8 * c:8 * c + 8],
                                                 spare[0][:, 0:64].rearrange("p (t a h) -> p t a h", a=2, h=8),
                                                 ACT.Copy).then_inc(band_taken.sem, 1)
                        if s in SETTLE and (it + SETTLE[s][0]).real(BATCHES):
                            at, g = it + SETTLE[s][0], SETTLE[s][1]
                            if k == 1:
                                act.wait_ge(*band_shifted.after(at, g - 1))
                                act.wait_ge(*band_values.after(at - 1, g + 1))
                                nc.scalar.activation(band_exp[g][:, :, :, :], band_arg[g][:, :, :, :], ACT.Exp,
                                                     scale=SCALE).then_inc(band_exped.sem, 1)
                            if k == 2:
                                job = {1: 5, 3: 11, 5: 19, 7: 25}[s]
                                act.wait_ge(*m_turned.after(at, g - 1))
                                before = (at, g - 1) if g else (at - 1, 3)
                                act.wait_ge(*m_row[before[1]].after(before[0] - (before[1] == 0), 0))
                                nc.scalar.activation(mT[:, :], spare[job % 2][0:HEADS, 0:P // 2].bitcast(F16),
                                                     ACT.Copy).then_inc(m_copied.sem, 1)
                                act.wait_ge(*m_copied.after(at, g - 1))
                                act.dma_start(q_stack[g][64:65, :, :].rearrange("p h (t q) -> p (h t) q", q=P),
                                              mT[:, :]).then_inc(m_row[g].sem, 16)
                        if s == 3 and k in (4, 5) and late.real(BATCHES):
                            c = k - 4
                            act.wait_ge(*y_turned.after(it, c))
                            nc.scalar.activation(yT[:, c, :], spare[(13, 14)[c] % 2][:, :], ACT.Copy).then_inc(yT_stored.sem, 1)
                        if (s, k) in ((5, 6), (6, 4)) and nxt.real(BATCHES):
                            c = s - 5
                            act.wait_ge(*ffn_k_made.after(it, c))
                            act.wait_ge(*ffn_k_taken.after(late, c))
                            nc.scalar.activation(ffn_act[:, c, :], spare[1][:, :], ACT.Relu).then_inc(relu_made.sem, 1)
                        if (s, k) in ((6, 6), (7, 4)) and nxt.real(BATCHES):
                            j = s - 6
                            act.wait_ge(*gate_made.after(it, j))
                            act.wait_ge(*ffn_added.after(it if j else late, 1 - j))
                            nc.scalar.activation(gate[:, 2 * j:2 * j + 2, :],
                                                 spare[0][:, :].rearrange("p (t n) -> p t n", t=2),
                                                 ACT.Tanh, scale=0.5).then_inc(gate_taken.sem, 1)
                        if k in FILL_SLOT and it.real(BATCHES):
                            f, g, i0 = FILL_SLOT[k], s // 2, 2 * (s % 2)
                            b, parts = FILLS[f]
                            act.wait_ge(*scored.after(it, 5 * s + f))
                            if f == 0 and s % 2 == 0:
                                act.wait_ge(*o_added.after(it, g - 1))
                            if f == 4:
                                dst = probs[g % 2][:, i0:i0 + 2, KEY_AT[2]:KEY_AT[2] + 256]
                                src = fill_bank[b][:, :].rearrange("p (h w) -> p h w", h=2)
                            else:
                                h, j, _ = parts[0]
                                dst = probs[g % 2][:, i0 + h, KEY_AT[j]:KEY_AT[j] + 512]
                                src = fill_bank[b][:, :]
                            nc.scalar.activation(dst, src, ACT.Exp, scale=SCALE).then_inc(probs_made.sem, 1)

            iterations(act, body)

        @block.vector
        def _(dve):
            for g in range(NG):
                nc.vector.memset(q_stack[g][64:128, :, :], 0.0)
                nc.vector.memset(k_stack[g][64:128, :, :], 0.0).then_inc(vconsts_ready, 1)
            dve.wait_ge(vconsts_ready, NG)
            for g in range(NG):
                nc.vector.memset(k_stack[g][64:65, :, :], M_UNIT).then_inc(vconsts_ready, 1)
            dve.wait_ge(rows_in, 8 * 16)
            per_head = "p (h d) -> p h d"
            for n, r in enumerate((0, 2, 1)):
                nc.vector.tensor_tensor(rows[0:1, 1 + n, :].rearrange(per_head, d=HD),
                                        b_k_row[:, :].rearrange(per_head, d=HD),
                                        rel_row[:, r, :].unsqueeze(1).to_broadcast([1, HEADS, HD]), ALU.add)
            nc.vector.tensor_scalar(rows[0:1, 4:6, :], mu_rows[:, :, :], -1.0, 1.0, ALU.mult,
                                    ALU.add).then_inc(rows_ready, 1)
            for r in range(3):
                nc.vector.tensor_tensor(v_bias[:, r, :].rearrange(per_head, d=HD),
                                        b_v_all[:, :].rearrange(per_head, d=HD),
                                        rel_v_all[:, r, :].unsqueeze(1).to_broadcast([P, HEADS, HD]),
                                        ALU.add).then_inc(vconsts_ready, 1)
            dve.wait_ge(vconsts_ready, 2 * NG + 3)
            dve.wait_ge(consts_ready, 15)
            dve.wait_ge(setup_taken, 4)

            def take_heads(it, s):
                at, g = it + TAIL[s][0], TAIL[s][1]
                src = spare[0][:, :].rearrange("p (t h d) -> p t h d", t=TB, h=GROUP)
                dve.wait_ge(*heads_turned.after(at, g + 2))
                dve.wait_ge(*band_values.after(at, g + 1))
                dve.wait_ge(*y_made.after(at, g + 1))
                nc.vector.tensor_tensor(denom[:, :, :], src[:, :, :, HD],
                                        band_sum[:, :, :].rearrange("p h t -> p t h"),
                                        ALU.add).then_inc(head_step.sem, 1)
                nc.vector.tensor_tensor(num[:, :, :, :], src[:, :, :, 0:HD], band_v[:, :, :, :],
                                        ALU.add).then_inc(heads_taken.sem, 1)
                dve.wait_ge(*head_step.after(at, 2 * g + 4))
                nc.vector.reciprocal(inv[:, :, :], denom[:, :, :]).then_inc(head_step.sem, 1)
                dve.wait_ge(*heads_taken.after(at, g + 2))
                dve.wait_ge(*head_step.after(at, 2 * g + 5))
                nc.vector.tensor_tensor(y[:, :, GROUP * g * HD:GROUP * (g + 1) * HD].rearrange("p t (h d) -> p t h d", d=HD),
                                        num[:, :, :, :], inv[:, :, :].unsqueeze(3).to_broadcast([P, TB, GROUP, HD]),
                                        ALU.mult).then_inc(y_made.sem, 1)

            def inverse_root(it):
                bits = mybir.dt.int32
                nc.vector.tensor_scalar(var_eps[:, :], mean_var[:, :, 1], EPS, None, ALU.add).then_inc(root_step.sem, 1)
                dve.wait_ge(*root_step.after(it, 0))
                nc.vector.tensor_scalar(rstd[:, :].bitcast(bits), var_eps[:, :].bitcast(bits), 1, None,
                                        ALU.logical_shift_right).then_inc(root_step.sem, 1)
                dve.wait_ge(*root_step.after(it, 1))
                nc.vector.tensor_scalar(rstd[:, :].bitcast(bits), rstd[:, :].bitcast(bits), -1, ROOT_GUESS, ALU.mult,
                                        ALU.add).then_inc(root_step.sem, 1)
                for n in range(NEWTON):
                    dve.wait_ge(*root_step.after(it, 3 * n + 2))
                    nc.vector.scalar_tensor_tensor(root_a[:, :], rstd[:, :], -0.5, rstd[:, :], ALU.mult,
                                                   ALU.mult).then_inc(root_step.sem, 1)
                    dve.wait_ge(*root_step.after(it, 3 * n + 3))
                    nc.vector.tensor_tensor(root_b[:, :], root_a[:, :], var_eps[:, :],
                                            ALU.mult).then_inc(root_step.sem, 1)
                    dve.wait_ge(*root_step.after(it, 3 * n + 4))
                    done = ln_step if n == NEWTON - 1 else root_step
                    nc.vector.scalar_tensor_tensor(rstd[:, :], root_b[:, :], 1.5, rstd[:, :], ALU.add,
                                                   ALU.mult).then_inc(done.sem, 1)

            def settle_max(it, s):
                at, g = it + SETTLE[s][0], SETTLE[s][1]
                pair = band[at.parity][:, :, :, GROUP * g:GROUP * (g + 1)]
                own, prev = (pair[:, :, n, :].rearrange("p t h -> p h t") for n in range(2))
                if g == 0:
                    dve.wait_ge(*band_taken.after(at - 1, 1))
                    nc.vector.memset(band[at.parity][0:1, 0, 1, :], MASKED).then_inc(first_masked.sem, 1)
                    dve.wait_ge(*first_masked.after(at - 1, 0))
                dve.wait_ge(*max_taken.after(at, 8 * (2 * g + 1 - LEAD) + 7))
                nc.vector.tensor_tensor(m_own[:, :, :], mx[g][:, :, :], own, ALU.max).then_inc(m_step.sem, 1)
                dve.wait_ge(*m_step.after(at, 2 * (g - 1)))
                nc.vector.tensor_tensor(m_all[:, :, :], m_own[:, :, :], prev, ALU.max).then_inc(m_step.sem, 1)
                dve.wait_ge(*m_step.after(at, 2 * (g - 1) + 1))
                nc.vector.tensor_scalar(m16[g][:, :, :], m_all[:, :, :], -1.0 / M_UNIT, None,
                                        ALU.mult).then_inc(m_rounded.sem, 1)
                dve.wait_ge(*m_rounded.after(at, g - 1))
                dve.wait_ge(*band_exped.after(at - 1, g - 1))
                for n, part in enumerate((own, prev)):
                    last = nc.vector.scalar_tensor_tensor(band_arg[g][:, n], m16[g][:, :, :], M_UNIT, part,
                                                          ALU.mult, ALU.add)
                last.then_inc(band_shifted.sem, 1)

            def body(it):
                nxt, late = it + 1, it - 1
                for s in range(STEPS):
                    for k in range(SLOTS):
                        if s in TAIL and k == 2 and (it + TAIL[s][0]).real(BATCHES):
                            take_heads(it, s)
                        if s in SETTLE and k == 0 and (it + SETTLE[s][0]).real(BATCHES):
                            settle_max(it, s)
                        if (s, k) in ((0, 3), (7, 6)) and (it + s // 7).real(BATCHES):
                            at, j, pos = (it, 1, 0) if s == 0 else (nxt, 0, 1)
                            dve.wait_ge(*ffn_v_made.after(it, pos))
                            dve.wait_ge(*gate_ready.after(at - 1, j))
                            nc.vector.tensor_tensor(gate[:, 2 * j:2 * j + 2, :], gate[:, 2 * j:2 * j + 2, :],
                                                    spare[1][:, :].rearrange("p (t n) -> p t n", t=2),
                                                    ALU.mult).then_inc(ffn_v_taken.sem, 1)
                        if s in (1, 2) and k in (5, 6) and nxt.real(BATCHES):
                            c = s - 1
                            src = spare[(6, 9)[c] % 2]
                            if k == 5:
                                dve.wait_ge(*k_high.after(it, c))
                                dve.wait_ge(*q_taken.after(it, c))
                                dve.wait_ge(*split_stored[c].after(late, 3))
                                nc.vector.scalar_tensor_tensor(kl[:, c, :], src[:, :], cols[:, 1, c:c + 1], kh[:, c, :],
                                                               ALU.add, ALU.subtract).then_inc(k_low.sem, 1)
                                nc.vector.scalar_tensor_tensor(band_prod[:, 0, c, :], src[:, :], cols[:, 2, c:c + 1],
                                                               qf[:, c, :], ALU.add, ALU.mult)
                            else:
                                nc.vector.scalar_tensor_tensor(band_prod[:, 1, c, 1:SEQ], src[:, 0:SEQ - 1],
                                                               cols[:, 3, c:c + 1], qf[:, c, 1:SEQ],
                                                               ALU.add, ALU.mult).then_inc(k_taken.sem, 1)
                        if (s, k) in ((3, 2), (4, 0)) and nxt.real(BATCHES):
                            dst, row = (xr, 4) if s == 3 else (xk, 5)
                            for c in range(CH):
                                dve.wait_ge(*dx_made.after(it, c))
                                nc.vector.scalar_tensor_tensor(dst[:, c, :], dx[:, c, :], cols[:, row, c:c + 1],
                                                               xf[:, c, 1:SEQ + 1], ALU.mult,
                                                               ALU.add).then_inc(mixed.sem, 1)
                        if (s, k) in ((3, 7), (5, 4)) and nxt.real(BATCHES):
                            j = (s - 3) // 2
                            job = (15, 20)[j]
                            src = spare[job % 2][:, :].rearrange("p (t h d) -> p t h d", t=2, h=HEADS)
                            dve.wait_ge(*v_made.after(it, j))
                            if j == 0:
                                dve.wait_ge(*v_shifted.after(late, 2))
                                dve.wait_ge(*band_values.after(it, 0))
                            ts = slice(2 * j, 2 * j + 2)
                            for r, dst in ((0, v0[nxt.parity][:, ts, :, 0:HD]),
                                           (1, v_next[:, ts, :].rearrange("p t (h d) -> p t h d", d=HD)),
                                           (2, v_own[nxt.parity][:, ts, :].rearrange("p t (h d) -> p t h d", d=HD))):
                                bias = v_bias[:, r, :].rearrange("p (h d) -> p h d", d=HD).unsqueeze(1)
                                last = nc.vector.tensor_tensor(dst, src, bias.to_broadcast([P, 2, HEADS, HD]), ALU.add)
                            last.then_inc(v_stored.sem, 1)
                        if s == 4 and k in (4, 6) and late.real(BATCHES):
                            j = (k - 4) // 2
                            dve.wait_ge(*o_made.after(it, j))
                            dve.wait_ge(*ffn_added.after(late, 0))
                            w = w_sum[late.parity][:, 2 * j:2 * j + 2, :]
                            nc.vector.tensor_tensor(w, w,
                                                    spare[(17, 18)[j] % 2][:, :].rearrange("p (t n) -> p t n", t=2),
                                                    ALU.add).then_inc(summed.sem, 1)
                        if (s, k) in ((5, 7), (6, 5)) and nxt.real(BATCHES):
                            c = s - 5
                            dve.wait_ge(*relu_made.after(it, c))
                            nc.vector.scalar_tensor_tensor(ffn_act[:, c, :], spare[1][:, :], 0.0, ffn_act[:, c, :],
                                                           ALU.max, ALU.mult).then_inc(ffn_k_taken.sem, 1)
                        if (s, k) == (6, 0) and has_ln(it):
                            dve.wait_ge(*x_loaded.after(it, 0))
                            dve.wait_ge(*xn_made.after(late, 0))
                            for t in range(TB):
                                last = nc.vector.bn_stats(stats[:, t, :], x_nat[it.parity][:, t, :])
                            last.then_inc(ln_step.sem, 1)
                            dve.wait_ge(*ln_step.after(it, 0))
                            dve.sem_inc(dve_waited, 1)
                            for t in range(TB):
                                last = nc.vector.bn_aggr(mean_var[:, t, :], stats[:, t, :])
                            last.then_inc(ln_aggr.sem, 1)
                            dve.wait_ge(*ln_aggr.after(it, 0))
                            inverse_root(it)
                        at, pair = max_target(it, s)
                        if at.real(BATCHES):
                            g, i, qb = pair // 2, 2 * (pair % 2) + k // 4, TB - 1 - k % 4
                            width = P * (qb + 1)
                            dve.wait_ge(*max_scored.after(it, 8 * s + k))
                            dve.sem_inc(dve_waited, 1)
                            nc.vector.tensor_tensor_reduce(out=spill[k % 2][:, 0:width], in0=max_bank[k % 2][:, 0:width],
                                                           in1=key_mask[:, SEQ - width:SEQ], scale=1.0,
                                                           scalar=MASKED, op0=ALU.add, op1=ALU.max,
                                                           accum_out=mx[g][:, i, qb:qb + 1]).then_inc(max_taken.sem, 1)

            first_masked = count("first_masked", 1, (-1, 0))
            ln_aggr = count("ln_aggr", 1, (-2, 0))
            iterations(dve, body)

        @block.tensor
        def _(pe):
            pe.wait_ge(weights_in, 7 * 16)
            pe.wait_ge(consts_ready, 15)
            for n in range(3):
                for ci in range(CH):
                    for di in range(CH):
                        at = E * di + P * ci
                        last = nc.tensor.transpose(bank[2 + n][:, E * ci + P * di:E * ci + P * (di + 1)],
                                                   probs[0][:, n, at:at + P], ident[:, :])
                last.then_inc(turned_weights, 1)
            pe.wait_ge(rows_ready, 1)
            for r in range(6):
                for c in range(CH):
                    last = nc.tensor.matmul(o_bank[:, CH * r + c:CH * r + c + 1], rows[0:1, r, P * c:P * (c + 1)],
                                            one[:, :], start=True, stop=True)
            last.then_inc(cols_made, 1)
            pe.wait_ge(setup_taken, 4)
            pe.wait_ge(vconsts_ready, 2 * NG)

            def turn_heads(it, s, job):
                at, g = it + TAIL[s][0], TAIL[s][1]
                pe.wait_ge(*o_taken.after(at, g + 2))
                pe.wait_ge(*spare_free(job, it))
                for t in range(TB):
                    last = nc.tensor.transpose(spare[job % 2][:, P * t:P * (t + 1)], oT[:, P * t:P * (t + 1)], ident[:, :])
                last.then_inc(heads_turned.sem, 1)

            def turn_max(it, s, job):
                at, g = it + SETTLE[s][0], SETTLE[s][1]
                pe.wait_ge(*m_rounded.after(at, g - 1))
                pe.wait_ge(*spare_free(job, it))
                nc.tensor.transpose(spare[job % 2][0:HEADS, 0:P // 2].bitcast(F16),
                                    m16[g][:, :, :].rearrange("p h t -> p (h t)"), ident16[:, :]).then_inc(m_turned.sem, 1)

            def channels(job, c, weights, src, done):
                for ci in range(CH):
                    last = nc.tensor.matmul(spare[job % 2][:, :], weights[:, ci, P * c:P * (c + 1)], src(ci),
                                            start=(ci == 0), stop=(ci == CH - 1))
                last.then_inc(done.sem, 1)

            def tokens(job, j, weights, src, done):
                for t in range(2):
                    for ci in range(CH):
                        last = nc.tensor.matmul(spare[job % 2][:, E * t:E * (t + 1)], src(ci, 2 * j + t),
                                                weights[:, ci, :], start=(ci == 0), stop=(ci == CH - 1))
                last.then_inc(done.sem, 1)

            def block_of(tile, first=0):
                return lambda ci, t: tile[:, ci, first + P * t:first + P * (t + 1)]

            def spare_work(it, s, k):
                nxt, late = it + 1, it - 1
                ahead = nxt.real(BATCHES)
                if (s, k) == (0, 1) and late.real(BATCHES):
                    turn_heads(it, s, 0)
                if (s, k) == (0, 2) and it.real(BATCHES):
                    pe.wait_ge(*ffn_k_taken.after(late, 1))
                    pe.wait_ge(*spare_free(1, it))
                    tokens(1, 1, w_fvT, block_of(ffn_act), ffn_v_made)
                if s == 0 and k in (3, 4) and ahead:
                    c = k - 3
                    pe.wait_ge(*xn_made.after(late, 0))
                    pe.wait_ge(*spare_free(2 + c, it))
                    for t in range(TB):
                        last = nc.tensor.transpose(spare[c][:, P * t:P * (t + 1)], xn[:, t, P * c:P * (c + 1)], ident[:, :])
                    last.then_inc(xn_turned.sem, 1)
                if (s, k) in ((0, 6), (1, 4)) and ahead:
                    c = s
                    pe.wait_ge(*xf_stored.after(it, 1))
                    pe.wait_ge(*spare_free((4, 7)[c], it))
                    channels((4, 7)[c], c, w_q, lambda ci: xf[:, ci, 1:SEQ + 1], q_made)
                if (s, k) == (1, 1) and it.real(BATCHES):
                    turn_max(it, s, 5)
                if (s, k) in ((1, 2), (2, 2)) and ahead:
                    c = s - 1
                    pe.wait_ge(*spare_free((6, 9)[c], it))
                    channels((6, 9)[c], c, w_k, lambda ci: xf[:, ci, 1:SEQ + 1], k_made)
                if (s, k) == (2, 1) and late.real(BATCHES):
                    turn_heads(it, s, 8)
                if (s, k) in ((2, 5), (3, 2)) and ahead:
                    c = s - 2
                    job = (10, 12)[c]
                    pe.wait_ge(*k_taken.after(it, c))
                    pe.wait_ge(*spare_free(job, it))
                    for t in range(TB):
                        for n in range(2):
                            last = nc.tensor.matmul(spare[0][:, 16 * t + 8 * n:16 * t + 8 * n + 8],
                                                    band_prod[:, n, c, P * t:P * (t + 1)], head_ones[:, :],
                                                    start=True, stop=True)
                    last.then_inc(band_summed.sem, 1)
                if (s, k) == (3, 1) and it.real(BATCHES):
                    turn_max(it, s, 11)
                if s == 3 and k in (3, 4) and late.real(BATCHES):
                    c = k - 3
                    job = (13, 14)[c]
                    pe.wait_ge(*y_made.after(late, 5))
                    pe.wait_ge(*spare_free(job, it))
                    for t in range(TB):
                        last = nc.tensor.transpose(spare[job % 2][:, P * t:P * (t + 1)], y[:, t, P * c:P * (c + 1)], ident[:, :])
                    last.then_inc(y_turned.sem, 1)
                if (s, k) in ((3, 6), (5, 2)) and ahead:
                    j = (s - 3) // 2
                    job = (15, 20)[j]
                    pe.wait_ge(*spare_free(job, it))
                    tokens(job, j, w_v, block_of(xf, 1), v_made)
                if (s, k) == (4, 1) and it.real(BATCHES):
                    turn_heads(it, s, 16)
                if s == 4 and k in (2, 4) and late.real(BATCHES):
                    j = (k - 2) // 2
                    job = (17, 18)[j]
                    pe.wait_ge(*yT_stored.after(it, 1))
                    pe.wait_ge(*spare_free(job, it))
                    tokens(job, j, w_o, block_of(yT), o_made)
                if (s, k) == (5, 1) and it.real(BATCHES):
                    turn_max(it, s, 19)
                if (s, k) in ((5, 5), (6, 2)) and ahead:
                    c = s - 5
                    job = (21, 23)[c]
                    pe.wait_ge(*mixed.after(it, 3))
                    pe.wait_ge(*spare_free(job, it))
                    channels(job, c, w_fkT, lambda ci: xk[:, ci, :], ffn_k_made)
                if (s, k) == (6, 1) and it.real(BATCHES):
                    turn_heads(it, s, 22)
                if (s, k) in ((6, 5), (7, 2)) and ahead:
                    j = s - 6
                    job = (24, 26)[j]
                    pe.wait_ge(*spare_free(job, it))
                    tokens(job, j, w_rT, block_of(xr), gate_made)
                if (s, k) == (7, 1) and ahead:
                    turn_max(it, s, 25)
                if (s, k) == (7, 5) and ahead:
                    pe.wait_ge(*ffn_k_taken.after(it, 1))
                    pe.wait_ge(*spare_free(27, it))
                    tokens(27, 0, w_fvT, block_of(ffn_act), ffn_v_made)

            def body(it):
                for s in range(STEPS):
                    for k in range(SLOTS):
                        at, pair = max_target(it, s)
                        if at.real(BATCHES):
                            g, i, qb = pair // 2, 2 * (pair % 2) + k // 4, TB - 1 - k % 4
                            if pair % 2 == 0 and k == 0:
                                pe.wait_ge(*stack_loaded[g].after(at if g == 3 else at - 1, 5))
                            pe.wait_ge(*max_taken.after(it, 8 * s + k - 2))
                            nc.tensor.matmul(max_bank[k % 2][:, 0:P * (qb + 1)], q_stack[g][:, i, P * qb:P * (qb + 1)],
                                             k_stack[g][:, i, 0:P * (qb + 1)], start=True,
                                             stop=True).then_inc(max_scored.sem, 1)
                        if k in FILL_SLOT and it.real(BATCHES):
                            f, g, i0 = FILL_SLOT[k], s // 2, 2 * (s % 2)
                            b, parts = FILLS[f]
                            if f == 0 and s % 2 == 0:
                                pe.wait_ge(*m_row[g].after(it - 1 if g == 0 else it, 0))
                            pe.wait_ge(*probs_made.after(it, 5 * s + f - FILL_BACK[f]))
                            for h, j, col in parts:
                                last = nc.tensor.matmul(fill_bank[b][:, col:col + SEQ - P * j],
                                                        k_stack[g][:, i0 + h, P * j:P * (j + 1)],
                                                        q_stack[g][:, i0 + h, P * j:SEQ], start=True, stop=True)
                            last.then_inc(scored.sem, 1)
                        at = it if s >= 2 else it - 1
                        if k in (2, 5) and at.real(BATCHES):
                            g = (s - 2) // 2 % NG
                            j = 2 * (s % 2) + (k - 2) // 3
                            if j == 0:
                                pe.wait_ge(*probs_masked.after(at, 2 * g + 1))
                                pe.wait_ge(*o_taken.after(at, g + 1))
                                if g == 0:
                                    pe.wait_ge(*v_stored.after(at - 1, 1))
                            for i in range(GROUP):
                                last = nc.tensor.matmul(o_bank[32 * i:32 * (i + 1), P * j:SEQ],
                                                        v0[at.parity][:, j, GROUP * g + i, :],
                                                        probs[g % 2][:, i, KEY_AT[j]:KEY_AT[j] + SEQ - P * j],
                                                        start=(j == 0), stop=(j == TB - 1), skip_group_check=True)
                            if j == TB - 1:
                                last.then_inc(o_added.sem, 1)
                        spare_work(it, s, k)

            iterations(pe, body)


_INS = ["L0_attn_x", "L0_attn_W_q", "L0_attn_b_q", "L0_attn_W_k", "L0_attn_b_k", "L0_attn_W_v", "L0_attn_b_v",
        "L0_attn_W_o", "L0_attn_b_o", "L0_attn_rel_k_table", "L0_attn_rel_v_table", "L0_ffn_W_r", "L0_ffn_W_k",
        "L0_ffn_W_v", "L0_ffn_mu_r", "L0_ffn_mu_k"]


def kernel(**inputs):
    import numpy as _np
    import concourse.bacc as _bacc
    from concourse import mybir as _mybir
    from concourse.bass_utils import run_bass_kernel_spmd as _run

    nc = _bacc.Bacc("TRN2", target_bir_lowering=False, num_devices=1, dynamic_dma_scratch_size=4096)
    arrays, args = {}, []
    for name in _INS:
        a = _np.ascontiguousarray(inputs[name])
        arrays[f"in_{name}_dram"] = a
        args.append(nc.dram_tensor(f"in_{name}_dram", a.shape, _mybir.dt.from_np(a.dtype), kind="ExternalInput").ap())
    shape = inputs["L0_attn_x"].shape
    args.append(nc.dram_tensor("out_0_dram", shape, _mybir.dt.float32, kind="ExternalOutput").ap())
    rwkv_attention_block(nc, *args)
    r = _run(nc, [arrays], core_ids=[0])
    return r.results[0]["out_0_dram"]
```

```python
from contextlib import ExitStack

import concourse.bass as bass
from concourse import mybir

F32 = mybir.dt.float32
F16 = mybir.dt.float16
ALU = mybir.AluOpType
ACT = mybir.ActivationFunctionType

P = 128
HEADS, HD = 16, 16
CH = 2
GROUP = 4
STEPS = 8
SLOTS = 8
LEAD = 3
SCALE = 0.25
M_UNIT = 64.0
MASKED = -1e30
EPS = 1e-5
ROOT_GUESS = 0x5F3759DF
NEWTON = 3

KEY_AT = [768, 0, 512, 384]
KEY_STEP = 384
HEAD_COLS = 1280
FILLS = [
    [(0, 0, 0)],
    [(0, 1, 0), (0, 3, 384)],
    [(1, 0, 0)],
    [(1, 1, 0), (1, 3, 384)],
    [(0, 2, 0), (1, 2, 256)],
]
FILL_SLOT = {0: 0, 1: 1, 3: 2, 4: 3, 6: 4}
MAX_BANK = [n % 3 for n in range(STEPS * SLOTS - 1)] + [1]

JOBS = [
    ("heads", 2, -1, 0, 0, [1]),
    ("xf", 0, 1, 0, 1, [3]),
    ("xf", 1, 1, 1, 0, [4]),
    ("ffn_v", 1, 0, 0, 1, [5, 6, 7, 8]),
    ("q", 0, 1, 0, 0, [9, 11]),
    ("m", 1, 0, 0, 1, [11]),
    ("k", 0, 1, 0, 1, [13, 15]),
    ("q", 1, 1, 1, 0, [16, 19]),
    ("heads", 3, -1, 1, 1, [21]),
    ("k", 1, 1, 1, 0, [22, 24]),
    ("m", 2, 0, 1, 1, [25]),
    ("v", 0, 1, 0, 1, [27, 28, 29, 29]),
    ("band", 0, 1, 0, 0, [29]),
    ("yT", 0, -1, 0, 0, [31]),
    ("yT", 1, -1, 1, 0, [33]),
    ("heads", 0, 0, 2, 1, [33]),
    ("o", 0, -1, 0, 0, [35, 36, 37, 38]),
    ("o", 1, -1, 1, 1, [39, 40, 41, 42]),
    ("m", 3, 0, 2, 0, [41]),
    ("v", 1, 1, 1, 0, [43, 44, 45, 45]),
    ("ffn_k", 0, 1, 0, 1, [46, 47]),
    ("heads", 1, 0, 3, 0, [49]),
    ("ffn_k", 1, 1, 1, 1, [51, 53]),
    ("gate", 0, 1, 0, 0, [52, 54, 55, 56]),
    ("m", 0, 1, 3, 1, [58]),
    ("ffn_v", 0, 1, 1, 0, [58, 59, 60, 61]),
    ("gate", 1, 1, 1, 1, [61, 62, 63, 63]),
]
BANK_OF = {(what, which): bank for what, which, _, _, bank, _ in JOBS}


class Batch:

    def __init__(self, offset, register=None):
        self.offset, self.register = offset, register

    def __add__(self, n):
        return Batch(self.offset + n, self.register)

    def __sub__(self, n):
        return self + -n

    @property
    def parity(self):
        return self.offset % 2

    def real(self, batches):
        return self.register is not None or 0 <= self.offset < batches

    def index(self):
        return self.offset if self.register is None else self.register * 2 + self.offset


class Count:

    def __init__(self, sem, n, first, unit=1):
        self.sem, self.n, self.first, self.unit = sem, n, first, unit

    def after(self, it, pos):
        fixed = (self.n * (it.offset - self.first[0]) + pos - self.first[1] + 1) * self.unit
        if it.register is None:
            return self.sem, max(fixed, 0)
        assert fixed > 0, "an event before the first, in the loop"
        return self.sem, it.register * (2 * self.n * self.unit) + fixed

    def happened(self, it, pos):
        return it.register is not None or (it.offset, pos) >= self.first


def rwkv_attention_block(nc, x, W_q, b_q, W_k, b_k, W_v, b_v, W_o, b_o, rel_k, rel_v, W_r, W_fk, W_fv,
                         mu_r, mu_k, out):
    BATCHES, SEQ, E = x.shape
    TB = SEQ // P
    NG = HEADS // GROUP
    assert E == CH * P and SEQ == 512 and HEADS * HD == E and BATCHES == 8

    x_rows = x.rearrange("b (t p) e -> b p t e", p=P)
    out_rows = out.rearrange("b (t p) e -> b p t e", p=P)

    with ExitStack() as ctx:
        def sb(name, shape, dt=F32):
            return ctx.enter_context(nc.sbuf_tensor(name, shape, dt))

        def sem(name):
            return ctx.enter_context(nc.semaphore(name))

        w_q, w_k, w_v, w_o = (sb(f"w_{n}", [P, CH, E]) for n in "qkvo")
        w_rT, w_fkT, w_fvT = (sb(n, [P, CH, E]) for n in ("w_rT", "w_fkT", "w_fvT"))
        rows = sb("rows", [1, 6, E])
        rel_row = sb("rel_row", [1, 3, HD])
        b_k_row = sb("b_k_row", [1, E])
        mu_rows = sb("mu_rows", [1, 2, E])
        cols = sb("cols", [P, 6, CH])
        rel_v_all = sb("rel_v_all", [P, 3, HD])
        b_v_all = sb("b_v_all", [P, E])
        b_o_all = sb("b_o_all", [P, E])
        v_bias = sb("v_bias", [P, 3, E])
        ident = sb("ident", [P, P])
        ident16 = sb("ident16", [P, P], F16)
        head_ones = sb("head_ones", [P, 8])
        one = sb("one", [1, 1])
        key_mask = sb("key_mask", [P, SEQ])
        x_nat = [sb(f"x_nat{i}", [P, TB, E]) for i in range(2)]
        w_sum = [sb(f"w_sum{i}", [P, TB, E]) for i in range(2)]
        stats = sb("stats", [P, TB, 6])
        mean_var = sb("mean_var", [P, TB, 2])
        rstd, var_eps, root_a, root_b, neg_mean = (sb(n, [P, TB]) for n in ("rstd", "var_eps", "root_a", "root_b", "neg_mean"))
        xn = sb("xn", [P, TB, E])
        xf = sb("xf", [P, CH, SEQ + 1])
        dx = sb("dx", [P, CH, SEQ])
        xr = sb("xr", [P, CH, SEQ])
        xk = dx
        qf = sb("qf", [P, CH, SEQ])
        qh, ql, kh, kl = (sb(n, [P, CH, SEQ], F16) for n in ("qh", "ql", "kh", "kl"))
        band_prod = sb("band_prod", [P, 2, CH, SEQ])
        band = [sb(f"band{i}", [P, TB, 2, HEADS]) for i in range(2)]
        v0 = [sb(f"v0_{i}", [P, TB, HEADS, 2 * HD]) for i in range(2)]
        v_own = [sb(f"v_own{i}", [P, TB, E]) for i in range(2)]
        v_prev = [sb(f"v_prev{i}", [P, TB, E]) for i in range(2)]
        v_next = sb("v_next", [P, TB, E])
        ffn_act = sb("ffn_act", [P, CH, SEQ])
        gate = sb("gate", [P, TB, E])
        q_stack = [sb(f"q_stack{g}", [P, GROUP, SEQ], F16) for g in range(NG)]
        k_stack = [sb(f"k_stack{g}", [P, GROUP, SEQ], F16) for g in range(NG)]
        probs = [sb(f"probs{i}", [P, GROUP, HEAD_COLS]) for i in range(2)]
        spill = [sb(f"spill{i}", [P, SEQ], F16) for i in range(3)]
        mx = [sb(f"mx{g}", [P, GROUP, TB]) for g in range(NG)]
        beside = sb("beside", [P, TB, HEADS])
        m16 = [sb(f"m16_{g}", [P, GROUP, TB], F16) for g in range(NG)]
        mT = sb("mT", [HEADS, P], F16)
        band_arg = [sb(f"band_arg{g}", [P, 2, GROUP, TB]) for g in range(NG)]
        band_exp = [sb(f"band_exp{g}", [P, 2, GROUP, TB]) for g in range(NG)]
        band_sum = sb("band_sum", [P, GROUP, TB])
        band_a = sb("band_a", [P, TB, GROUP, HD])
        band_b = sb("band_b", [P, TB, GROUP, HD])
        band_v = sb("band_v", [P, TB, GROUP, HD])
        oT = sb("oT", [P, SEQ])
        denom = sb("denom", [P, TB, GROUP])
        inv = sb("inv", [P, TB, GROUP])
        num = sb("num", [P, TB, GROUP, HD])
        y = sb("y", [P, TB, E])
        yT = sb("yT", [P, CH, SEQ])

        split_q = [nc.dram_tensor(f"split_q{c}", (2 * P, SEQ), F16, kind="Internal").ap() for c in range(CH)]
        split_k = [nc.dram_tensor(f"split_k{c}", (2 * P, SEQ), F16, kind="Internal").ap() for c in range(CH)]

        bank = [ctx.enter_context(nc.psum_tensor(f"bank{i}", [P, 512], F32)) for i in range(8)]
        max_bank, fill_bank, o_bank, spare = bank[0:3], bank[3:5], bank[5], bank[6:8]

        weights_in, rows_in = sem("weights_in"), sem("rows_in")
        consts_ready, vconsts_ready, turned_weights, cols_made = (
            sem(n) for n in ("consts_ready", "vconsts_ready", "turned_weights", "cols_made"))
        setup_taken, rows_ready = sem("setup_taken"), sem("rows_ready")

        pool_waited, dve_waited, sp_waited = sem("pool_waited"), sem("dve_waited"), sem("sp_waited")

        def count(name, n, first, unit=1):
            return Count(sem(name), n, first, unit)

        x_loaded = count("x_loaded", 1, (-2, 0), 16)
        ln_step = count("ln_step", 2, (-2, 0))
        centred = count("centred", TB, (-2, 0))
        root_step = count("root_step", 3 * NEWTON + 3, (-2, 0))
        xn_made = count("xn_made", 1, (-2, 0))
        xn_turned = count("xn_turned", 2, (-1, 0))
        xf_stored = count("xf_stored", 2, (-1, 0))
        q_made = count("q_made", 2, (-1, 0))
        q_taken = count("q_taken", 2, (-1, 0))
        q_low = count("q_low", 2, (-1, 0))
        k_made = count("k_made", 2, (-1, 0))
        k_high = count("k_high", 2, (-1, 0))
        k_low = count("k_low", 2, (-1, 0))
        k_taken = count("k_taken", 2, (-1, 0))
        split_stored = [count(f"split_stored{c}", 4, (-1, 0), 16) for c in range(CH)]
        stack_loaded = [count(f"stack_loaded{g}", 6, (0 if g == 3 else -1, 0), 16) for g in range(NG)]
        band_summed = count("band_summed", 1, (-1, 0))
        band_taken = count("band_taken", 1, (-1, 0))
        v_made = count("v_made", 2, (-1, 0))
        v_stored = count("v_stored", 2, (-1, 0))
        v_shifted = count("v_shifted", 3, (-1, 0), 16)
        dx_made = count("dx_made", 2, (-1, 0))
        mixed = count("mixed", 4, (-1, 0))
        ffn_k_made = count("ffn_k_made", 2, (-1, 0))
        relu_made = count("relu_made", 2, (-1, 0))
        ffn_k_taken = count("ffn_k_taken", 2, (-1, 0))
        gate_made = count("gate_made", 2, (-1, 0))
        gate_taken = count("gate_taken", 2, (-1, 0))
        gate_ready = count("gate_ready", 2, (-1, 1))
        ffn_v_made = count("ffn_v_made", 2, (-1, 1))
        ffn_v_taken = count("ffn_v_taken", 2, (-1, 1))
        ffn_added = count("ffn_added", 2, (-1, 1))
        residual_copied = count("residual_copied", 2, (-1, 0))
        max_scored = count("max_scored", 64, (-1, 40))
        max_taken = count("max_taken", 64, (-1, 40))
        beside_made = count("beside_made", 3, (-1, 0))
        m_rounded = count("m_rounded", 4, (-1, 3))
        band_shifted = count("band_shifted", 4, (-1, 3))
        band_exped = count("band_exped", 4, (-1, 3))
        m_turned = count("m_turned", 4, (-1, 3))
        m_copied = count("m_copied", 4, (-1, 3))
        m_row = [count(f"m_row{g}", 1, (-1 if g == 0 else 0, 0), 16) for g in range(NG)]
        scored = count("scored", 40, (0, 0))
        probs_made = count("probs_made", 40, (0, 0))
        diagonals_masked = count("diagonals_masked", 8, (0, 0))
        probs_masked = count("probs_masked", 8, (0, 0))
        o_added = count("o_added", 4, (0, 1))
        o_taken = count("o_taken", 4, (0, 2))
        band_step = count("band_step", 12, (0, 3))
        band_values = count("band_values", 4, (0, 1))
        heads_turned = count("heads_turned", 4, (0, 2))
        heads_taken = count("heads_taken", 4, (0, 2))
        head_step = count("head_step", 8, (0, 4))
        y_made = count("y_made", 4, (0, 2))
        y_turned = count("y_turned", 2, (1, 0))
        yT_stored = count("yT_stored", 2, (1, 0))
        o_made = count("o_made", 2, (1, 0))
        summed = count("summed", 2, (1, 0))
        out_stored = [count(f"out_stored{j}", 1, (1, 0), 16) for j in range(2)]

        last_read = dict(heads=heads_taken, ffn_v=ffn_v_taken, xf=xf_stored, q=q_taken, m=m_copied, k=k_taken,
                         band=band_taken, yT=yT_stored, v=v_stored, o=summed, ffn_k=ffn_k_taken, gate=gate_taken)

        def spare_free(job, it):
            n, at, bank = job - 1, it, JOBS[job][4]
            while True:
                if n < 0:
                    n, at = n + len(JOBS), at - 1
                what, _, ahead, pos, b, _ = JOBS[n]
                if b == bank and (at.offset < -1 or (at + ahead).real(BATCHES)):
                    return last_read[what].after(at, pos)
                n -= 1

        def iterations(eng, body):
            for b in (-2, -1, 0):
                body(Batch(b))
            with eng.Fori(0, 3) as i:
                body(Batch(1, i))
                body(Batch(2, i))
            for b in (7, 8):
                body(Batch(b))

        def has_ln(it):
            return it.register is not None or it.offset <= 6

        def max_target(it, s):
            return (it, s + LEAD) if s + LEAD < STEPS else (it + 1, s + LEAD - STEPS)

        def max_back(n):
            back = 1
            while MAX_BANK[n - back] != MAX_BANK[n]:
                back += 1
            return back

        SETTLE = {1: (0, 1), 3: (0, 2), 5: (0, 3), 7: (1, 0)}
        TAIL = {0: (-1, 2), 2: (-1, 3), 4: (0, 0), 6: (0, 1)}
        TAKE = (2, 22, 34, 50)
        BAND = {1: (-1, 3), 3: (0, 0), 5: (0, 1), 7: (0, 2)}

        block = ctx.enter_context(nc.Block())

        @block.sync
        def _(sp):
            for src, dst in ((W_q, w_q), (W_k, w_k), (W_v, w_v), (W_o, w_o)):
                sp.dma_start(dst[:, :, :], src.rearrange("(c p) n -> p c n", p=P)).then_inc(weights_in, 16)
            for n, src in enumerate((W_r, W_fk, W_fv)):
                sp.dma_start(probs[0][:, n, 0:CH * E].rearrange("p (c n) -> p c n", c=CH),
                             src.rearrange("(c p) n -> p c n", p=P)).then_inc(weights_in, 16)

            def load_stack(it, g):
                c, half = g // 2, g % 2
                q_src = split_q[c][half * P:(half + 1) * P, :]
                k_src = split_k[c][half * P:(half + 1) * P, :]
                sp.wait_ge(*split_stored[c].after(it, 3))
                sp.sem_inc(sp_waited, 1)
                if it.register is not None or it.offset >= 0:
                    sp.wait_ge(*scored.after(it, 10 * g + 9))
                both = "(h r) t -> r h t"
                sp.dma_start(q_stack[g][0:32, :, :], q_src.rearrange(both, r=32)).then_inc(stack_loaded[g].sem, 16)
                sp.dma_start(k_stack[g][0:32, :, :], k_src.rearrange(both, r=32)).then_inc(stack_loaded[g].sem, 16)
                sp.dma_start(k_stack[g][32:64, :, :], k_src.rearrange(both, r=32)).then_inc(stack_loaded[g].sem, 16)
                halves = q_src.rearrange("(h l e) t -> l e h t", l=2, e=HD)
                sp.dma_start(q_stack[g][32:48, :, :], halves[1]).then_inc(stack_loaded[g].sem, 16)
                sp.dma_start(q_stack[g][48:64, :, :], halves[0]).then_inc(stack_loaded[g].sem, 16)
                sp.dma_start(q_stack[g][64:65, :, :], k_stack[g][65:66, :, :]).then_inc(stack_loaded[g].sem, 16)

            def store_split(it, c):
                for n, (src, dst, half, ready) in enumerate((
                        (qh, split_q, 0, q_taken), (ql, split_q, 1, q_low),
                        (kh, split_k, 0, k_high), (kl, split_k, 1, k_low))):
                    if n == 0 and (it.register is not None or it.offset >= 0):
                        for g in (2 * c, 2 * c + 1):
                            sp.wait_ge(*stack_loaded[g].after(it if g == 3 else it - 1, 5))
                            sp.sem_inc(sp_waited, 1)
                    sp.wait_ge(*ready.after(it, c))
                    sp.dma_start(dst[c].rearrange("(h l e) t -> h l e t", l=2, e=HD)[:, half, :, :],
                                 src[:, c, :]).then_inc(split_stored[c].sem, 16)

            def body(it):
                nxt, late = it + 1, it - 1
                if it.real(BATCHES):
                    load_stack(late, 3)
                if has_ln(it):
                    if it.register is not None or it.offset > -2:
                        sp.wait_ge(*ln_step.after(late, 0))
                        sp.sem_inc(sp_waited, 1)
                    if it.register is not None or it.offset >= 0:
                        sp.wait_ge(*residual_copied.after(late, 1))
                    ahead = it + 2
                    where = ahead.offset if it.register is None else ahead.index() % BATCHES
                    sp.dma_start(x_nat[it.parity][:, :, :], x_rows[bass.ds(where, 1)].rearrange("o p t e -> p (o t) e")
                                 if it.register is not None else x_rows[where]).then_inc(x_loaded.sem, 16)
                if nxt.real(BATCHES):
                    store_split(it, 0)
                    load_stack(it, 0)
                    store_split(it, 1)
                    load_stack(it, 1)
                if late.real(BATCHES):
                    for j in range(2):
                        sp.wait_ge(*summed.after(it, j))
                        at = late.index()
                        dst = (out_rows[bass.ds(at, 1)].rearrange("o p t e -> p (o t) e")
                               if it.register is not None else out_rows[at])
                        sp.dma_start(dst[:, 2 * j:2 * j + 2, :], w_sum[late.parity][:, 2 * j:2 * j + 2, :]).then_inc(out_stored[j].sem, 16)
                if nxt.real(BATCHES):
                    sp.wait_ge(*v_stored.after(it, 1))
                    sp.sem_inc(sp_waited, 1)
                    sp.wait_ge(*band_values.after(it, 0))
                    prev = v_prev[nxt.parity]
                    sp.dma_start(prev[1:113, :, :], v_next[0:112, :, :]).then_inc(v_shifted.sem, 16)
                    sp.dma_start(prev[113:128, :, :], v_next[112:127, :, :]).then_inc(v_shifted.sem, 16)
                    sp.dma_start(prev[0:1, 1:TB, :], v_next[127:128, 0:TB - 1, :]).then_inc(v_shifted.sem, 16)
                    load_stack(it, 2)

            iterations(sp, body)
            for j in range(2):
                sp.wait_ge(*out_stored[j].after(Batch(BATCHES), 0))

        @block.gpsimd
        def _(pool):
            for part, src in ((rows[0:1, 0, :], b_q), (b_k_row[:, :], b_k), (mu_rows[0:1, 0, :], mu_r),
                              (mu_rows[0:1, 1, :], mu_k)):
                pool.dma_start(part, src.rearrange("(o n) -> o n", o=1)).then_inc(rows_in, 16)
            pool.dma_start(rel_row[:, :, :], rel_k[0:3, :].rearrange("(o r) d -> o r d", o=1)).then_inc(rows_in, 16)
            pool.dma_start(rel_v_all[:, :, :],
                           rel_v[0:3, :].rearrange("(o r) d -> o r d", o=1).to_broadcast([P, 3, HD])).then_inc(rows_in, 16)
            pool.dma_start(b_v_all[:, :], b_v.rearrange("(o n) -> o n", o=1).to_broadcast([P, E])).then_inc(rows_in, 16)
            pool.dma_start(b_o_all[:, :], b_o.rearrange("(o n) -> o n", o=1).to_broadcast([P, E])).then_inc(rows_in, 16)
            nc.gpsimd.memset(ident[:, :], 0.0).then_inc(consts_ready, 1)
            nc.gpsimd.memset(head_ones[:, :], 1.0).then_inc(consts_ready, 1)
            nc.gpsimd.memset(key_mask[:, :], 0.0).then_inc(consts_ready, 1)
            pool.wait_ge(consts_ready, 3)
            nc.gpsimd.affine_select(out=ident[:, :], in_=ident[:, :], compare_op=ALU.not_equal, fill=1.0,
                                    base=0, pattern=[[-1, P]], channel_multiplier=1).then_inc(consts_ready, 1)
            nc.gpsimd.affine_select(out=head_ones[:, :], in_=head_ones[:, :], compare_op=ALU.is_ge, fill=0.0,
                                    base=0, pattern=[[-HD, 8]], channel_multiplier=1).then_inc(consts_ready, 1)
            nc.gpsimd.affine_select(out=key_mask[:, :], in_=key_mask[:, :], compare_op=ALU.is_ge, fill=MASKED,
                                    base=SEQ - P - 2, pattern=[[-1, SEQ]], channel_multiplier=1).then_inc(consts_ready, 1)
            pool.wait_ge(consts_ready, 6)
            nc.gpsimd.affine_select(out=head_ones[:, :], in_=head_ones[:, :], compare_op=ALU.is_ge, fill=0.0,
                                    base=HD - 1, pattern=[[HD, 8]], channel_multiplier=-1).then_inc(consts_ready, 1)
            nc.gpsimd.tensor_copy(ident16[:, :], ident[:, :]).then_inc(consts_ready, 1)
            nc.gpsimd.memset(one[:, :], 1.0).then_inc(consts_ready, 1)
            nc.gpsimd.memset(xf[:, :, 0:1], 0.0).then_inc(consts_ready, 1)
            nc.gpsimd.memset(band_prod[:, 1, :, 0:1], 0.0).then_inc(consts_ready, 1)
            for i in range(2):
                nc.gpsimd.memset(v_prev[i][0:1, 0, :], 0.0).then_inc(consts_ready, 1)
                nc.gpsimd.memset(v0[i][:, :, :, HD:2 * HD], 1.0).then_inc(consts_ready, 1)

            def body(it):
                nxt = it + 1
                for s in range(STEPS):
                    if s == 0 and it.real(BATCHES):
                        pool.wait_ge(*gate_taken.after(it - 1, 1))
                        pool.sem_inc(pool_waited, 1)
                        g2 = gate[:, 2:4, :]
                        nc.gpsimd.tensor_scalar(g2, g2, 0.5, 0.5, ALU.mult, ALU.add).then_inc(gate_ready.sem, 1)
                    if s == 0 and nxt.real(BATCHES):
                        for c in range(CH):
                            pool.wait_ge(*xf_stored.after(it, c))
                            if c == 0:
                                pool.wait_ge(*ffn_k_made.after(it - 1, 1))
                            nc.gpsimd.tensor_tensor(dx[:, c, :], xf[:, c, 0:SEQ], xf[:, c, 1:SEQ + 1],
                                                    ALU.subtract).then_inc(dx_made.sem, 1)
                    if s == 1 and it.real(BATCHES):
                        pool.wait_ge(*ffn_v_taken.after(it, 0))
                        w = w_sum[it.parity][:, 2:4, :]
                        nc.gpsimd.tensor_tensor(w, w, gate[:, 2:4, :], ALU.add).then_inc(ffn_added.sem, 1)
                    if s in (1, 2) and nxt.real(BATCHES):
                        c = s - 1
                        pool.wait_ge(*q_taken.after(it, c))
                        pool.wait_ge(*split_stored[c].after(it - 1, 3))
                        nc.gpsimd.tensor_tensor(ql[:, c, :], qf[:, c, :], qh[:, c, :],
                                                ALU.subtract).then_inc(q_low.sem, 1)
                    if s in BAND and (it + BAND[s][0]).real(BATCHES):
                        at, g = it + BAND[s][0], BAND[s][1]
                        pos = g + 1
                        e_own = band_exp[g][:, 0].rearrange("p h t -> p t h")
                        e_prev = band_exp[g][:, 1].rearrange("p h t -> p t h")
                        hs = slice(GROUP * g * HD, GROUP * (g + 1) * HD)
                        own = v_own[at.parity][:, :, hs].rearrange("p t (h d) -> p t h d", d=HD)
                        prev = v_prev[at.parity][:, :, hs].rearrange("p t (h d) -> p t h d", d=HD)
                        wide = [P, TB, GROUP, HD]
                        pool.wait_ge(*band_exped.after(at, g - 1))
                        pool.wait_ge(*v_stored.after(at - 1, 1))
                        pool.wait_ge(*v_shifted.after(at - 1, 2))
                        pool.wait_ge(*heads_taken.after(at, g + 1))
                        nc.gpsimd.tensor_tensor(band_sum[:, :, :], band_exp[g][:, 0], band_exp[g][:, 1],
                                                ALU.add).then_inc(band_step.sem, 1)
                        nc.gpsimd.tensor_tensor(band_a[:, :, :, :], own, e_own.unsqueeze(3).to_broadcast(wide),
                                                ALU.mult).then_inc(band_step.sem, 1)
                        nc.gpsimd.tensor_tensor(band_b[:, :, :, :], prev, e_prev.unsqueeze(3).to_broadcast(wide),
                                                ALU.mult).then_inc(band_step.sem, 1)
                        pool.wait_ge(*band_step.after(at, 3 * pos + 2))
                        nc.gpsimd.tensor_tensor(band_v[:, :, :, :], band_a[:, :, :, :], band_b[:, :, :, :],
                                                ALU.add).then_inc(band_values.sem, 1)
                    if s in (5, 6) and nxt.real(BATCHES):
                        j = s - 5
                        pool.wait_ge(*out_stored[j].after(it, 0))
                        pool.wait_ge(*x_loaded.after(it - 1, 0))
                        w = w_sum[nxt.parity][:, 2 * j:2 * j + 2, :]
                        nc.gpsimd.tensor_tensor(w, x_nat[nxt.parity][:, 2 * j:2 * j + 2, :],
                                                b_o_all[:, :].unsqueeze(1).to_broadcast([P, 2, E]),
                                                ALU.add).then_inc(residual_copied.sem, 1)
                    if s == 7 and nxt.real(BATCHES):
                        pool.wait_ge(*gate_taken.after(it, 0))
                        pool.sem_inc(pool_waited, 1)
                        g2 = gate[:, 0:2, :]
                        nc.gpsimd.tensor_scalar(g2, g2, 0.5, 0.5, ALU.mult, ALU.add).then_inc(gate_ready.sem, 1)
                    if it.real(BATCHES):
                        g, i0 = s // 2, 2 * (s % 2)
                        pool.wait_ge(*probs_made.after(it, 5 * s + 4))
                        pool.sem_inc(pool_waited, 1)
                        pr = probs[g % 2][:, i0:i0 + 2, :]
                        for h in range(2):
                            part = pr[:, h, 0:3 * KEY_STEP].rearrange("p (j w) -> p j w", w=KEY_STEP)[:, :, 0:P + 1]
                            last = nc.gpsimd.affine_select(out=part, in_=part, compare_op=ALU.is_ge, fill=0.0, base=-2,
                                                           pattern=[[0, 3], [1, P + 1]], channel_multiplier=-1)
                        last.then_inc(diagonals_masked.sem, 1)
                        pool.wait_ge(*diagonals_masked.after(it, s))
                        pool.sem_inc(pool_waited, 1)
                        part = pr[:, :, KEY_AT[2]:KEY_AT[2] + P + 1]
                        nc.gpsimd.affine_select(out=part, in_=part, compare_op=ALU.is_ge, fill=0.0, base=-2,
                                                pattern=[[0, 2], [1, P + 1]],
                                                channel_multiplier=-1).then_inc(probs_masked.sem, 1)
                    if s == 7 and nxt.real(BATCHES):
                        pool.wait_ge(*ffn_v_taken.after(it, 1))
                        w = w_sum[nxt.parity][:, 0:2, :]
                        nc.gpsimd.tensor_tensor(w, w, gate[:, 0:2, :], ALU.add).then_inc(ffn_added.sem, 1)

            iterations(pool, body)

        @block.scalar
        def _(act):
            for n, dst in enumerate((w_rT, w_fkT, w_fvT)):
                act.wait_ge(turned_weights, n + 1)
                nc.scalar.activation(dst[:, :, :], bank[2 + n][:, :].rearrange("p (c n) -> p c n", c=CH),
                                     ACT.Copy).then_inc(setup_taken, 1)
            act.wait_ge(cols_made, 1)
            nc.scalar.activation(cols[:, :, :], o_bank[:, 0:12].rearrange("p (a c) -> p a c", c=CH),
                                 ACT.Copy).then_inc(setup_taken, 1)
            act.wait_ge(setup_taken, 4)

            def take_gate(it, j):
                act.wait_ge(*gate_made.after(it, j))
                act.wait_ge(*ffn_added.after(it if j else it - 1, 1 - j))
                nc.scalar.activation(gate[:, 2 * j:2 * j + 2, :],
                                     spare[BANK_OF["gate", j]][:, :].rearrange("p (t n) -> p t n", t=2),
                                     ACT.Tanh, scale=0.5).then_inc(gate_taken.sem, 1)

            def body(it):
                nxt, late = it + 1, it - 1
                for s in range(STEPS):
                    for k in range(SLOTS):
                        n = SLOTS * s + k
                        if k == 0 and s in TAIL and (it + TAIL[s][0]).real(BATCHES):
                            at, g = it + TAIL[s][0], TAIL[s][1]
                            act.wait_ge(*o_added.after(at, g + 1))
                            act.wait_ge(*heads_turned.after(at, g + 1))
                            nc.scalar.activation(oT[:, :], o_bank[:, :], ACT.Copy).then_inc(o_taken.sem, 1)
                        if n in (4, 5) and nxt.real(BATCHES):
                            c = n - 4
                            act.wait_ge(*xn_turned.after(it, c))
                            act.wait_ge(*mixed.after(late, 3))
                            nc.scalar.activation(xf[:, c, 1:SEQ + 1], spare[BANK_OF["xf", c]][:, :],
                                                 ACT.Copy).then_inc(xf_stored.sem, 1)
                        if n in (12, 21) and nxt.real(BATCHES):
                            c = n // 21
                            src = spare[BANK_OF["q", c]]
                            act.wait_ge(*q_made.after(it, c))
                            act.wait_ge(*k_taken.after(late, c))
                            act.wait_ge(*split_stored[c].after(late, 3))
                            nc.scalar.activation(qf[:, c, :], src[:, :], ACT.Identity, bias=cols[:, 0, c:c + 1])
                            nc.scalar.activation(qh[:, c, :], src[:, :], ACT.Identity,
                                                 bias=cols[:, 0, c:c + 1]).then_inc(q_taken.sem, 1)
                        if n in (16, 25) and nxt.real(BATCHES):
                            c = n // 25
                            act.wait_ge(*k_made.after(it, c))
                            act.wait_ge(*split_stored[c].after(late, 3))
                            nc.scalar.activation(kh[:, c, :], spare[BANK_OF["k", c]][:, :], ACT.Identity,
                                                 bias=cols[:, 1, c:c + 1]).then_inc(k_high.sem, 1)
                        if n == 30 and nxt.real(BATCHES):
                            act.wait_ge(*band_summed.after(it, 0))
                            nc.scalar.activation(band[nxt.parity][:, :, :, :],
                                                 spare[BANK_OF["band", 0]][:, 0:P].rearrange("p (t a h) -> p t a h", a=2, h=HEADS),
                                                 ACT.Copy).then_inc(band_taken.sem, 1)
                        if s in SETTLE and (it + SETTLE[s][0]).real(BATCHES):
                            at, g = it + SETTLE[s][0], SETTLE[s][1]
                            if k == 2:
                                act.wait_ge(*band_shifted.after(at, g - 1))
                                act.wait_ge(*band_values.after(at - 1, g + 1))
                                nc.scalar.activation(band_exp[g][:, :, :, :], band_arg[g][:, :, :, :], ACT.Exp,
                                                     scale=SCALE).then_inc(band_exped.sem, 1)
                            if n == {1: 12, 3: 26, 5: 42, 7: 59}[s]:
                                act.wait_ge(*m_turned.after(at, g - 1))
                                before = (at, g - 1) if g else (at - 1, 3)
                                act.wait_ge(*m_row[before[1]].after(before[0] - (before[1] == 0), 0))
                                nc.scalar.activation(mT[:, :], spare[BANK_OF["m", g]][0:HEADS, 0:P // 2].bitcast(F16),
                                                     ACT.Copy).then_inc(m_copied.sem, 1)
                                act.wait_ge(*m_copied.after(at, g - 1))
                                act.dma_start(q_stack[g][64:65, :, :].rearrange("p h (t q) -> p (h t) q", q=P),
                                              mT[:, :]).then_inc(m_row[g].sem, 16)
                        if n in (32, 34) and late.real(BATCHES):
                            c = (n - 32) // 2
                            act.wait_ge(*y_turned.after(it, c))
                            nc.scalar.activation(yT[:, c, :], spare[BANK_OF["yT", c]][:, :],
                                                 ACT.Copy).then_inc(yT_stored.sem, 1)
                        if n in (48, 54) and nxt.real(BATCHES):
                            c = (n - 48) // 6
                            act.wait_ge(*ffn_k_made.after(it, c))
                            act.wait_ge(*ffn_k_taken.after(late, c))
                            nc.scalar.activation(ffn_act[:, c, :], spare[BANK_OF["ffn_k", c]][:, :],
                                                 ACT.Relu).then_inc(relu_made.sem, 1)
                        if n in range(50, 55) and has_ln(it):
                            if n < 50 + TB:
                                t = n - 50
                                if t == 0:
                                    act.wait_ge(*ln_step.after(it, 1))
                                    act.wait_ge(*xn_turned.after(it, 1))
                                nc.scalar.activation(xn[:, t, :], x_nat[it.parity][:, t, :], ACT.Identity,
                                                     bias=neg_mean[:, t:t + 1]).then_inc(centred.sem, 1)
                            if n > 50:
                                t = n - 51
                                act.wait_ge(*centred.after(it, t))
                                last = nc.scalar.activation(xn[:, t, :], xn[:, t, :], ACT.Copy, scale=rstd[:, t:t + 1])
                                if t == TB - 1:
                                    last.then_inc(xn_made.sem, 1)
                        if n == 57 and nxt.real(BATCHES):
                            take_gate(it, 0)
                        if k in FILL_SLOT and it.real(BATCHES):
                            f, g, i0 = FILL_SLOT[k], s // 2, 2 * (s % 2)
                            b, parts = (5 * s + f) % 2, FILLS[f]
                            act.wait_ge(*scored.after(it, 5 * s + f))
                            if f == 0 and s % 2 == 0:
                                act.wait_ge(*o_added.after(it, g - 1))
                            if f == 4:
                                dst = probs[g % 2][:, i0:i0 + 2, KEY_AT[2]:KEY_AT[2] + 256]
                                src = fill_bank[b][:, :].rearrange("p (h w) -> p h w", h=2)
                            else:
                                h, j, _ = parts[0]
                                dst = probs[g % 2][:, i0 + h, KEY_AT[j]:KEY_AT[j] + 512]
                                src = fill_bank[b][:, :]
                            nc.scalar.activation(dst, src, ACT.Exp, scale=SCALE).then_inc(probs_made.sem, 1)
                if nxt.real(BATCHES):
                    take_gate(it, 1)

            iterations(act, body)

        @block.vector
        def _(dve):
            for g in range(NG):
                nc.vector.memset(q_stack[g][64:128, :, :], 0.0)
                nc.vector.memset(k_stack[g][64:128, :, :], 0.0).then_inc(vconsts_ready, 1)
            dve.wait_ge(vconsts_ready, NG)
            for g in range(NG):
                nc.vector.memset(k_stack[g][64:65, :, :], M_UNIT).then_inc(vconsts_ready, 1)
            dve.wait_ge(rows_in, 8 * 16)
            per_head = "p (h d) -> p h d"
            for n, r in enumerate((0, 2, 1)):
                nc.vector.tensor_tensor(rows[0:1, 1 + n, :].rearrange(per_head, d=HD),
                                        b_k_row[:, :].rearrange(per_head, d=HD),
                                        rel_row[:, r, :].unsqueeze(1).to_broadcast([1, HEADS, HD]), ALU.add)
            nc.vector.tensor_scalar(rows[0:1, 4:6, :], mu_rows[:, :, :], -1.0, 1.0, ALU.mult,
                                    ALU.add).then_inc(rows_ready, 1)
            for r in range(3):
                nc.vector.tensor_tensor(v_bias[:, r, :].rearrange(per_head, d=HD),
                                        b_v_all[:, :].rearrange(per_head, d=HD),
                                        rel_v_all[:, r, :].unsqueeze(1).to_broadcast([P, HEADS, HD]),
                                        ALU.add).then_inc(vconsts_ready, 1)
            dve.wait_ge(vconsts_ready, 2 * NG + 3)
            dve.wait_ge(consts_ready, 15)
            dve.wait_ge(setup_taken, 4)

            def take_heads(it, s):
                at, g = it + TAIL[s][0], TAIL[s][1]
                src = spare[BANK_OF["heads", g]][:, :].rearrange("p (t h d) -> p t h d", t=TB, h=GROUP)
                dve.wait_ge(*heads_turned.after(at, g + 2))
                dve.wait_ge(*band_values.after(at, g + 1))
                dve.wait_ge(*y_made.after(at, g + 1))
                nc.vector.tensor_tensor(denom[:, :, :], src[:, :, :, HD],
                                        band_sum[:, :, :].rearrange("p h t -> p t h"),
                                        ALU.add).then_inc(head_step.sem, 1)
                nc.vector.tensor_tensor(num[:, :, :, :], src[:, :, :, 0:HD], band_v[:, :, :, :],
                                        ALU.add).then_inc(heads_taken.sem, 1)
                dve.wait_ge(*head_step.after(at, 2 * g + 4))
                nc.vector.reciprocal(inv[:, :, :], denom[:, :, :]).then_inc(head_step.sem, 1)
                dve.wait_ge(*heads_taken.after(at, g + 2))
                dve.wait_ge(*head_step.after(at, 2 * g + 5))
                nc.vector.tensor_tensor(y[:, :, GROUP * g * HD:GROUP * (g + 1) * HD].rearrange("p t (h d) -> p t h d", d=HD),
                                        num[:, :, :, :], inv[:, :, :].unsqueeze(3).to_broadcast([P, TB, GROUP, HD]),
                                        ALU.mult).then_inc(y_made.sem, 1)

            def root_step_at(it, n):
                bits = mybir.dt.int32
                dve.wait_ge(*(root_step.after(it, n - 1) if n else ln_aggr.after(it, 0)))
                if n == 0:
                    nc.vector.tensor_scalar(neg_mean[:, :], mean_var[:, :, 0], -1.0, None, ALU.mult)
                    made = nc.vector.tensor_scalar(var_eps[:, :], mean_var[:, :, 1], EPS, None, ALU.add)
                elif n == 1:
                    made = nc.vector.tensor_scalar(root_a[:, :].bitcast(bits), var_eps[:, :].bitcast(bits), 1, None,
                                                   ALU.logical_shift_right)
                elif n == 2:
                    made = nc.vector.tensor_scalar(rstd[:, :].bitcast(bits), root_a[:, :].bitcast(bits), -1,
                                                   ROOT_GUESS, ALU.mult, ALU.add)
                elif n % 3 == 0:
                    made = nc.vector.scalar_tensor_tensor(root_a[:, :], rstd[:, :], -0.5, rstd[:, :], ALU.mult, ALU.mult)
                elif n % 3 == 1:
                    made = nc.vector.tensor_tensor(root_b[:, :], root_a[:, :], var_eps[:, :], ALU.mult)
                else:
                    made = nc.vector.scalar_tensor_tensor(rstd[:, :], root_b[:, :], 1.5, rstd[:, :], ALU.add, ALU.mult)
                made.then_inc(root_step.sem, 1)
                if n == 3 * NEWTON + 2:
                    dve.wait_ge(*root_step.after(it, n))
                    dve.sem_inc(ln_step.sem, 1)

            def settle_max(it, s):
                at, g = it + SETTLE[s][0], SETTLE[s][1]
                apart = beside[:, :, GROUP * g:GROUP * (g + 1)].rearrange("p t h -> p h t")
                dve.wait_ge(*max_taken.after(at, 8 * (2 * g + 1 - LEAD) + 7))
                if g == 0:
                    dve.wait_ge(*beside_made.after(at - 1, 2))
                nc.vector.scalar_tensor_tensor(m16[g][:, :, :], mx[g][:, :, :], -1.0 / M_UNIT, apart,
                                               ALU.mult, ALU.min).then_inc(m_rounded.sem, 1)

            def prepare_band(it, n):
                scores = band[(it + 1).parity]
                if n == 0:
                    dve.wait_ge(*band_taken.after(it, 0))
                    made = nc.vector.memset(scores[0:1, 0, 1, :], MASKED)
                elif n == 1:
                    dve.wait_ge(*beside_made.after(it, 0))
                    made = nc.vector.tensor_tensor(beside[:, :, :], scores[:, :, 0, :], scores[:, :, 1, :], ALU.max)
                else:
                    dve.wait_ge(*beside_made.after(it, 1))
                    made = nc.vector.tensor_scalar(beside[:, :, :], beside[:, :, :], -1.0 / M_UNIT, None, ALU.mult)
                made.then_inc(beside_made.sem, 1)

            def shift_band(it, s):
                at, g = it + SETTLE[s][0], SETTLE[s][1]
                pair = band[at.parity][:, :, :, GROUP * g:GROUP * (g + 1)]
                dve.wait_ge(*m_rounded.after(at, g - 1))
                dve.wait_ge(*band_exped.after(at - 1, g - 1))
                for n in range(2):
                    last = nc.vector.scalar_tensor_tensor(band_arg[g][:, n], m16[g][:, :, :], M_UNIT,
                                                          pair[:, :, n, :].rearrange("p t h -> p h t"),
                                                          ALU.mult, ALU.add)
                last.then_inc(band_shifted.sem, 1)

            def body(it):
                nxt, late = it + 1, it - 1
                for s in range(STEPS):
                    for k in range(SLOTS):
                        n = SLOTS * s + k
                        if n in TAKE and (it + TAIL[s][0]).real(BATCHES):
                            take_heads(it, s)
                        if s in SETTLE and k < 2 and (it + SETTLE[s][0]).real(BATCHES):
                            (settle_max, shift_band)[k](it, s)
                        if n in (9, 62) and (it + n // 62).real(BATCHES):
                            at, j, pos = (it, 1, 0) if n == 9 else (nxt, 0, 1)
                            dve.wait_ge(*ffn_v_made.after(it, pos))
                            dve.wait_ge(*gate_ready.after(it, pos))
                            nc.vector.tensor_tensor(gate[:, 2 * j:2 * j + 2, :], gate[:, 2 * j:2 * j + 2, :],
                                                    spare[BANK_OF["ffn_v", j]][:, :].rearrange("p (t n) -> p t n", t=2),
                                                    ALU.mult).then_inc(ffn_v_taken.sem, 1)
                        if n in (17, 18, 19, 26, 27, 28) and nxt.real(BATCHES):
                            c, part = (n - 17) // 9, (n - 17) % 9
                            src = spare[BANK_OF["k", c]]
                            if part == 0:
                                dve.wait_ge(*k_high.after(it, c))
                                dve.wait_ge(*q_taken.after(it, c))
                                dve.wait_ge(*split_stored[c].after(late, 3))
                                nc.vector.scalar_tensor_tensor(kl[:, c, :], src[:, :], cols[:, 1, c:c + 1], kh[:, c, :],
                                                               ALU.add, ALU.subtract).then_inc(k_low.sem, 1)
                            elif part == 1:
                                dve.wait_ge(*band_summed.after(late, 0))
                                nc.vector.scalar_tensor_tensor(band_prod[:, 0, c, :], src[:, :], cols[:, 2, c:c + 1],
                                                               qf[:, c, :], ALU.add, ALU.mult)
                            else:
                                nc.vector.scalar_tensor_tensor(band_prod[:, 1, c, 1:SEQ], src[:, 0:SEQ - 1],
                                                               cols[:, 3, c:c + 1], qf[:, c, 1:SEQ],
                                                               ALU.add, ALU.mult).then_inc(k_taken.sem, 1)
                        if n in (11, 12, 13, 14) and nxt.real(BATCHES):
                            c = (n - 11) % 2
                            dst, row = (xr, 4) if n < 13 else (xk, 5)
                            dve.wait_ge(*dx_made.after(it, c))
                            if n >= 13:
                                dve.wait_ge(*mixed.after(it, c))
                            nc.vector.scalar_tensor_tensor(dst[:, c, :], dx[:, c, :], cols[:, row, c:c + 1],
                                                           xf[:, c, 1:SEQ + 1], ALU.mult,
                                                           ALU.add).then_inc(mixed.sem, 1)
                        if n in (30, 31, 32, 46, 47, 48) and nxt.real(BATCHES):
                            j, r = (n - 30) // 16, (n - 30) % 16
                            src = spare[BANK_OF["v", j]][:, :].rearrange("p (t h d) -> p t h d", t=2, h=HEADS)
                            if r == 0:
                                dve.wait_ge(*v_made.after(it, j))
                            if n == 30:
                                dve.wait_ge(*v_shifted.after(late, 2))
                                dve.wait_ge(*band_values.after(it, 0))
                            ts = slice(2 * j, 2 * j + 2)
                            dst = (v0[nxt.parity][:, ts, :, 0:HD],
                                   v_next[:, ts, :].rearrange("p t (h d) -> p t h d", d=HD),
                                   v_own[nxt.parity][:, ts, :].rearrange("p t (h d) -> p t h d", d=HD))[r]
                            bias = v_bias[:, r, :].rearrange("p (h d) -> p h d", d=HD).unsqueeze(1)
                            last = nc.vector.tensor_tensor(dst, src, bias.to_broadcast([P, 2, HEADS, HD]), ALU.add)
                            if r == 2:
                                last.then_inc(v_stored.sem, 1)
                        if n in (39, 43) and late.real(BATCHES):
                            j = (n - 39) // 4
                            dve.wait_ge(*o_made.after(it, j))
                            dve.wait_ge(*ffn_added.after(late, 0))
                            w = w_sum[late.parity][:, 2 * j:2 * j + 2, :]
                            nc.vector.tensor_tensor(w, w,
                                                    spare[BANK_OF["o", j]][:, :].rearrange("p (t n) -> p t n", t=2),
                                                    ALU.add).then_inc(summed.sem, 1)
                        if n in (49, 55) and nxt.real(BATCHES):
                            c = (n - 49) // 6
                            dve.wait_ge(*relu_made.after(it, c))
                            nc.vector.scalar_tensor_tensor(ffn_act[:, c, :], spare[BANK_OF["ffn_k", c]][:, :], 0.0,
                                                           ffn_act[:, c, :], ALU.max, ALU.mult).then_inc(ffn_k_taken.sem, 1)
                        if n in (33, 34, 36, 37) and has_ln(it):
                            t = (33, 34, 36, 37).index(n)
                            if t == 0:
                                dve.wait_ge(*x_loaded.after(it, 0))
                            last = nc.vector.bn_stats(stats[:, t, :], x_nat[it.parity][:, t, :])
                            if t == TB - 1:
                                last.then_inc(ln_step.sem, 1)
                        if n == 38 and has_ln(it):
                            dve.wait_ge(*xn_made.after(late, 0))
                            dve.wait_ge(*ln_step.after(it, 0))
                            dve.sem_inc(dve_waited, 1)
                            for t in range(TB):
                                last = nc.vector.bn_aggr(mean_var[:, t, :], stats[:, t, :])
                            last.then_inc(ln_aggr.sem, 1)
                        if n in range(39, 39 + 3 * NEWTON + 3) and has_ln(it):
                            root_step_at(it, n - 39)
                        if n in (51, 52, 53) and nxt.real(BATCHES):
                            prepare_band(it, n - 51)
                        at, pair = max_target(it, s)
                        if at.real(BATCHES):
                            g, i, qb = pair // 2, 2 * (pair % 2) + k // 4, TB - 1 - k % 4
                            width = P * (qb + 1)
                            dve.wait_ge(*max_scored.after(it, 8 * s + k))
                            dve.sem_inc(dve_waited, 1)
                            nc.vector.tensor_tensor_reduce(out=spill[MAX_BANK[n]][:, 0:width], in0=max_bank[MAX_BANK[n]][:, 0:width],
                                                           in1=key_mask[:, SEQ - width:SEQ], scale=1.0,
                                                           scalar=MASKED, op0=ALU.add, op1=ALU.max,
                                                           accum_out=mx[g][:, i, qb:qb + 1]).then_inc(max_taken.sem, 1)

            ln_aggr = count("ln_aggr", 1, (-2, 0))
            iterations(dve, body)

        @block.tensor
        def _(pe):
            pe.wait_ge(weights_in, 7 * 16)
            pe.wait_ge(consts_ready, 15)
            for n in range(3):
                for ci in range(CH):
                    for di in range(CH):
                        at = E * di + P * ci
                        last = nc.tensor.transpose(bank[2 + n][:, E * ci + P * di:E * ci + P * (di + 1)],
                                                   probs[0][:, n, at:at + P], ident[:, :])
                last.then_inc(turned_weights, 1)
            pe.wait_ge(rows_ready, 1)
            for r in range(6):
                for c in range(CH):
                    last = nc.tensor.matmul(o_bank[:, CH * r + c:CH * r + c + 1], rows[0:1, r, P * c:P * (c + 1)],
                                            one[:, :], start=True, stop=True)
            last.then_inc(cols_made, 1)
            pe.wait_ge(setup_taken, 4)
            pe.wait_ge(vconsts_ready, 2 * NG)

            def spare_work(it, job, n):
                what, which, ahead, pos, b, parts = JOBS[job]
                of, late, dst = it + ahead, it - 1, spare[b]
                token_blocks = dict(v=(w_v, xf, 1, v_made), o=(w_o, yT, 0, o_made), gate=(w_rT, xr, 0, gate_made),
                                    ffn_v=(w_fvT, ffn_act, 0, ffn_v_made))
                channel_blocks = dict(q=(w_q, xf, 1, q_made), k=(w_k, xf, 1, k_made), ffn_k=(w_fkT, xk, 0, ffn_k_made))
                if n == 0:
                    pe.wait_ge(*spare_free(job, it))
                if what in token_blocks:
                    if n == 0:
                        if what == "o":
                            pe.wait_ge(*yT_stored.after(it, 1))
                        if what == "ffn_v":
                            pe.wait_ge(*ffn_k_taken.after(it if which == 0 else late, 1))
                        if what == "gate":
                            pe.wait_ge(*mixed.after(it, 1))
                        if what == "v":
                            pe.wait_ge(*xf_stored.after(it, 1))
                    weights, src, first, done = token_blocks[what]
                    t, ci = n // 2, n % 2
                    at = first + P * (2 * which + t)
                    last = nc.tensor.matmul(dst[:, E * t:E * (t + 1)], src[:, ci, at:at + P], weights[:, ci, :],
                                            start=(ci == 0), stop=(ci == CH - 1))
                    if n == 3:
                        last.then_inc(done.sem, 1)
                elif what in channel_blocks:
                    if n == 0:
                        if what == "ffn_k":
                            pe.wait_ge(*mixed.after(it, 3))
                        else:
                            pe.wait_ge(*xf_stored.after(it, 1))
                    weights, src, first, done = channel_blocks[what]
                    last = nc.tensor.matmul(dst[:, :], weights[:, n, P * which:P * (which + 1)],
                                            src[:, n, first:first + SEQ], start=(n == 0), stop=(n == CH - 1))
                    if n == CH - 1:
                        last.then_inc(done.sem, 1)
                elif what == "heads":
                    pe.wait_ge(*o_taken.after(of, which + 2))
                    for t in range(TB):
                        last = nc.tensor.transpose(dst[:, P * t:P * (t + 1)], oT[:, P * t:P * (t + 1)], ident[:, :])
                    last.then_inc(heads_turned.sem, 1)
                elif what == "m":
                    pe.wait_ge(*m_rounded.after(of, which - 1))
                    nc.tensor.transpose(dst[0:HEADS, 0:P // 2].bitcast(F16),
                                        m16[which][:, :, :].rearrange("p h t -> p (h t)"),
                                        ident16[:, :]).then_inc(m_turned.sem, 1)
                elif what == "xf":
                    pe.wait_ge(*xn_made.after(late, 0))
                    for t in range(TB):
                        last = nc.tensor.transpose(dst[:, P * t:P * (t + 1)], xn[:, t, P * which:P * (which + 1)], ident[:, :])
                    last.then_inc(xn_turned.sem, 1)
                elif what == "yT":
                    pe.wait_ge(*y_made.after(late, 5))
                    for t in range(TB):
                        last = nc.tensor.transpose(dst[:, P * t:P * (t + 1)], y[:, t, P * which:P * (which + 1)], ident[:, :])
                    last.then_inc(y_turned.sem, 1)
                elif what == "band":
                    pe.wait_ge(*k_taken.after(it, 1))
                    for t in range(TB):
                        for a in range(2):
                            for c in range(CH):
                                at = 2 * HEADS * t + HEADS * a + 8 * c
                                last = nc.tensor.matmul(dst[:, at:at + 8], band_prod[:, a, c, P * t:P * (t + 1)],
                                                        head_ones[:, :], start=True, stop=True)
                    last.then_inc(band_summed.sem, 1)

            def body(it):
                for s in range(STEPS):
                    for k in range(SLOTS):
                        at, pair = max_target(it, s)
                        if at.real(BATCHES):
                            g, i, qb = pair // 2, 2 * (pair % 2) + k // 4, TB - 1 - k % 4
                            if pair % 2 == 0 and k == 0:
                                pe.wait_ge(*stack_loaded[g].after(at if g == 3 else at - 1, 5))
                            pe.wait_ge(*max_taken.after(it, 8 * s + k - max_back(8 * s + k)))
                            nc.tensor.matmul(max_bank[MAX_BANK[8 * s + k]][:, 0:P * (qb + 1)], q_stack[g][:, i, P * qb:P * (qb + 1)],
                                             k_stack[g][:, i, 0:P * (qb + 1)], start=True,
                                             stop=True).then_inc(max_scored.sem, 1)
                        if k in FILL_SLOT and it.real(BATCHES):
                            f, g, i0 = FILL_SLOT[k], s // 2, 2 * (s % 2)
                            b, parts = (5 * s + f) % 2, FILLS[f]
                            if f == 0 and s % 2 == 0:
                                pe.wait_ge(*m_row[g].after(it - 1 if g == 0 else it, 0))
                            pe.wait_ge(*probs_made.after(it, 5 * s + f - 2))
                            for h, j, col in parts:
                                last = nc.tensor.matmul(fill_bank[b][:, col:col + SEQ - P * j],
                                                        k_stack[g][:, i0 + h, P * j:P * (j + 1)],
                                                        q_stack[g][:, i0 + h, P * j:SEQ], start=True, stop=True)
                            last.then_inc(scored.sem, 1)
                        at = it if s >= 2 else it - 1
                        if k in (2, 5) and at.real(BATCHES):
                            g = (s - 2) // 2 % NG
                            j = 2 * (s % 2) + (k - 2) // 3
                            if j == 0:
                                pe.wait_ge(*probs_masked.after(at, 2 * g + 1))
                                pe.wait_ge(*o_taken.after(at, g + 1))
                                if g == 0:
                                    pe.wait_ge(*v_stored.after(at - 1, 1))
                            for i in range(GROUP):
                                last = nc.tensor.matmul(o_bank[32 * i:32 * (i + 1), P * j:SEQ],
                                                        v0[at.parity][:, j, GROUP * g + i, :],
                                                        probs[g % 2][:, i, KEY_AT[j]:KEY_AT[j] + SEQ - P * j],
                                                        start=(j == 0), stop=(j == TB - 1), skip_group_check=True)
                            if j == TB - 1:
                                last.then_inc(o_added.sem, 1)
                        for job, (_, _, ahead, _, _, slots) in enumerate(JOBS):
                            if (it + ahead).real(BATCHES):
                                for part, slot in enumerate(slots):
                                    if slot == 8 * s + k:
                                        spare_work(it, job, part)

            iterations(pe, body)


_INS = ["L0_attn_x", "L0_attn_W_q", "L0_attn_b_q", "L0_attn_W_k", "L0_attn_b_k", "L0_attn_W_v", "L0_attn_b_v",
        "L0_attn_W_o", "L0_attn_b_o", "L0_attn_rel_k_table", "L0_attn_rel_v_table", "L0_ffn_W_r", "L0_ffn_W_k",
        "L0_ffn_W_v", "L0_ffn_mu_r", "L0_ffn_mu_k"]


def kernel(**inputs):
    import numpy as _np
    import concourse.bacc as _bacc
    from concourse import mybir as _mybir
    from concourse.bass_utils import run_bass_kernel_spmd as _run

    nc = _bacc.Bacc("TRN2", target_bir_lowering=False, num_devices=1, dynamic_dma_scratch_size=4096)
    arrays, args = {}, []
    for name in _INS:
        a = _np.ascontiguousarray(inputs[name])
        arrays[f"in_{name}_dram"] = a
        args.append(nc.dram_tensor(f"in_{name}_dram", a.shape, _mybir.dt.from_np(a.dtype), kind="ExternalInput").ap())
    shape = inputs["L0_attn_x"].shape
    args.append(nc.dram_tensor("out_0_dram", shape, _mybir.dt.float32, kind="ExternalOutput").ap())
    rwkv_attention_block(nc, *args)
    r = _run(nc, [arrays], core_ids=[0])
    return r.results[0]["out_0_dram"]
```

```python
from contextlib import ExitStack

import numpy as np

import concourse.bass as bass
from concourse import mybir

F32 = mybir.dt.float32
F16 = mybir.dt.float16
F32R = mybir.dt.float32r
I32 = mybir.dt.int32
ALU = mybir.AluOpType
ACT = mybir.ActivationFunctionType

P = 128
HEADS, HD = 16, 16
CH = 2
GROUP = 4
STEPS = 8
SLOTS = 8
LEAD = 3
SCALE = 0.25
M_UNIT = 64.0
TWO_UNITS = float(np.full(2, M_UNIT, np.float16).view(np.float32)[0])
MASKED = -1e30
HIGH_BITS = -4096
EPS = 1e-5
ROOT_GUESS = 0x5F3759DF
NEWTON = 3

KEY_AT = [768, 0, 512, 384]
HEAD_COLS = 1280
FILLS = [
    [(0, 0, 0)],
    [(0, 3, 384), (0, 1, 0)],
    [(1, 0, 0)],
    [(1, 3, 384), (1, 1, 0)],
    [(0, 2, 0), (1, 2, 256)],
]
FILL_SLOT = {0: 0, 1: 1, 3: 2, 4: 3, 6: 4}
MAX_BANK = [n % 3 for n in range(STEPS * SLOTS - 1)] + [1]

JOBS = [
    ("xf", 0, 1, 0, 0, [0]),
    ("xf", 1, 1, 1, 1, [3]),
    ("heads", 2, -1, 0, 0, [4]),
    ("ffn_v", 1, 0, 0, 1, [5, 6, 7, 8]),
    ("q", 0, 1, 0, 0, [9, 9, 10, 10, 11, 11]),
    ("m", 1, 0, 0, 1, [11]),
    ("k", 0, 1, 0, 1, [13, 13, 14, 14, 15, 15]),
    ("q", 1, 1, 1, 0, [16, 16, 17, 17, 19, 19]),
    ("heads", 3, -1, 1, 1, [20]),
    ("k", 1, 1, 1, 0, [21, 21, 22, 22, 23, 23]),
    ("m", 2, 0, 1, 1, [25]),
    ("v", 0, 1, 0, 1, [28, 29, 30, 30]),
    ("pairs", 0, 1, 0, 0, [29]),
    ("band", 0, 1, 0, 0, [31]),
    ("yT", 0, -1, 0, 0, [33]),
    ("yT", 1, -1, 1, 1, [35]),
    ("heads", 0, 0, 2, 1, [37]),
    ("o", 0, -1, 0, 0, [37, 38, 39, 39]),
    ("o", 1, -1, 1, 1, [40, 41, 43, 43]),
    ("m", 3, 0, 2, 0, [41]),
    ("v", 1, 1, 1, 0, [43, 44, 45, 45]),
    ("ffn_k", 0, 1, 0, 1, [46, 46, 46, 47, 47, 47]),
    ("heads", 1, 0, 3, 0, [50]),
    ("ffn_k", 1, 1, 1, 1, [51, 51, 52, 52, 53, 53]),
    ("gate", 0, 1, 0, 0, [52, 54, 55, 56]),
    ("m", 0, 1, 3, 1, [58]),
    ("ffn_v", 0, 1, 1, 0, [58, 59, 60, 61]),
    ("gate", 1, 1, 1, 1, [61, 62, 63, 63]),
]
BANK_OF = {(what, which): bank for what, which, _, _, bank, _ in JOBS}


class Batch:

    def __init__(self, offset, register=None):
        self.offset, self.register = offset, register

    def __add__(self, n):
        return Batch(self.offset + n, self.register)

    def __sub__(self, n):
        return self + -n

    @property
    def parity(self):
        return self.offset % 2

    def real(self, batches):
        return self.register is not None or 0 <= self.offset < batches

    def is_first(self, offset):
        return self.register is None and self.offset == offset

    def index(self):
        return self.offset if self.register is None else self.register * 2 + self.offset


class Count:

    def __init__(self, sem, n, first, unit=1):
        self.sem, self.n, self.first, self.unit = sem, n, first, unit

    def after(self, it, pos):
        fixed = (self.n * (it.offset - self.first[0]) + pos - self.first[1] + 1) * self.unit
        if it.register is None:
            return self.sem, max(fixed, 0)
        assert fixed > 0, "an event before the first, in the loop"
        return self.sem, it.register * (2 * self.n * self.unit) + fixed


def rwkv_attention_block(nc, x, W_q, b_q, W_k, b_k, W_v, b_v, W_o, b_o, rel_k, rel_v, W_r, W_fk, W_fv,
                         mu_r, mu_k, out):
    BATCHES, SEQ, E = x.shape
    TB = SEQ // P
    NG = HEADS // GROUP
    assert E == CH * P and SEQ == 512 and HEADS * HD == E and BATCHES == 8

    x_rows = x.rearrange("b (t p) e -> b p t e", p=P)
    out_rows = out.rearrange("b (t p) e -> b p t e", p=P)

    with ExitStack() as ctx:
        def sb(name, shape, dt=F32):
            return ctx.enter_context(nc.sbuf_tensor(name, shape, dt))

        def sem(name):
            return ctx.enter_context(nc.semaphore(name))

        w_v, w_o, w_rT, w_fvT = (sb(n, [P, CH, E]) for n in ("w_v", "w_o", "w_rT", "w_fvT"))
        w_high = [sb(f"w_high_{n}", [P, CH, E], F32R) for n in ("q", "k", "fkT")]
        w_low = [sb(f"w_low_{n}", [P, CH, E], F32R) for n in ("q", "k", "fkT")]
        rel_row = sb("rel_row", [1, 3, HD])
        cols = sb("cols", [P, 6, CH])
        rel_v_all = sb("rel_v_all", [P, 3, HD])
        b_o_all = sb("b_o_all", [P, E])
        v_bias = sb("v_bias", [P, 3, E])
        ident = sb("ident", [P, P])
        ident16 = sb("ident16", [P, P], F16)
        head_ones = sb("head_ones", [P, 32])
        one = sb("one", [1, 1])
        key_mask = sb("key_mask", [P, SEQ])
        x_nat = [sb(f"x_nat{i}", [P, TB, E]) for i in range(2)]
        w_sum = [sb(f"w_sum{i}", [P, TB, E]) for i in range(2)]
        stats = sb("stats", [P, TB, 6])
        mean_var = sb("mean_var", [P, TB, 2])
        rstd, var_eps, root_a, root_b, neg_mean = (
            sb(n, [P, TB]) for n in ("rstd", "var_eps", "root_a", "root_b", "neg_mean"))
        turns = sb("turns", [P, TB * E])
        xn = turns[:, :].rearrange("p (t n) -> p t n", n=E)
        pair_rows = turns[:, 0:SEQ]
        yT = turns[:, :].rearrange("p (c n) -> p c n", n=SEQ)
        xf = sb("xf", [P, CH, SEQ + 1])
        dx = sb("dx", [P, CH, SEQ])
        xr = sb("xr", [P, CH, SEQ])
        xk = dx
        x_high, x_low = (sb(n, [P, CH, SEQ], F32R) for n in ("x_high", "x_low"))
        cut = sb("cut", [P, SEQ])
        qf = sb("qf", [P, CH, SEQ])
        kf = sb("kf", [P, CH, SEQ])
        qh, ql, kh, kl = (sb(n, [P, CH, SEQ], F16) for n in ("qh", "ql", "kh", "kl"))
        band_prod = sb("band_prod", [P, 2, CH, SEQ])
        band = [sb(f"band{i}", [P, TB, 2, HEADS]) for i in range(2)]
        v0 = [sb(f"v0_{i}", [P, TB, HEADS, 2 * HD]) for i in range(2)]
        v_own = [sb(f"v_own{i}", [P, TB, E]) for i in range(2)]
        v_prev = [sb(f"v_prev{i}", [P, TB, E]) for i in range(2)]
        v_next = band_prod[:, 0, :, :].rearrange("p c n -> p (c n)").rearrange("p (t n) -> p t n", n=E)
        ffn_act = sb("ffn_act", [P, CH, SEQ])
        gate = sb("gate", [P, TB, E])
        q_stack = [sb(f"q_stack{g}", [P, GROUP, SEQ], F16) for g in range(NG)]
        k_stack = [sb(f"k_stack{g}", [P, GROUP, SEQ], F16) for g in range(NG)]
        probs = [sb(f"probs{i}", [P, GROUP, HEAD_COLS]) for i in range(2)]
        staging = probs[1][:, :, :].rearrange("p h n -> p (h n)")
        rows = staging[0:1, 0:6 * E].rearrange("p (r n) -> p r n", n=E)
        b_k_row = staging[0:1, 6 * E:7 * E]
        mu_rows = staging[0:1, 7 * E:9 * E].rearrange("p (r n) -> p r n", n=E)
        b_v_all = staging[:, 9 * E:10 * E]
        mx = [sb(f"mx{g}", [P, GROUP, TB]) for g in range(NG)]
        beside = sb("beside", [P, TB, HEADS])
        m16 = [sb(f"m16_{g}", [P, GROUP, TB], F16) for g in range(NG)]
        mT = sb("mT", [HEADS, P], F16)
        band_arg = [sb(f"band_arg{g}", [P, 2, GROUP, TB]) for g in range(NG)]
        band_exp = [sb(f"band_exp{g}", [P, 2, GROUP, TB]) for g in range(NG)]
        band_sum = sb("band_sum", [P, GROUP, TB])
        band_a = sb("band_a", [P, TB, GROUP, HD])
        band_b = sb("band_b", [P, TB, GROUP, HD])
        band_v = sb("band_v", [P, TB, GROUP, HD])
        oT = sb("oT", [P, SEQ])
        denom = sb("denom", [P, TB, GROUP])
        inv = sb("inv", [P, TB, GROUP])
        num = sb("num", [P, TB, GROUP, HD])
        y = sb("y", [P, TB, E])

        split_q = [nc.dram_tensor(f"split_q{c}", (2 * P, SEQ), F16, kind="Internal").ap() for c in range(CH)]
        split_k = [nc.dram_tensor(f"split_k{c}", (2 * P, SEQ), F16, kind="Internal").ap() for c in range(CH)]

        bank = [ctx.enter_context(nc.psum_tensor(f"bank{i}", [P, 512], F32)) for i in range(8)]
        max_bank, fill_bank, o_bank, spare = bank[0:3], bank[3:5], bank[5], bank[6:8]

        weights_in = [sem(f"w_{n}_in") for n in ("q", "k", "v", "o", "ffn")]
        rows_in = sem("rows_in")
        consts_ready, vconsts_ready, turned_weights, cols_made = (
            sem(n) for n in ("consts_ready", "vconsts_ready", "turned_weights", "cols_made"))
        weights_taken, cols_taken, rows_ready, zeros_ready, w_halved = (
            sem(n) for n in ("weights_taken", "cols_taken", "rows_ready", "zeros_ready", "w_halved"))

        pool_waited, dve_waited, sp_waited = sem("pool_waited"), sem("dve_waited"), sem("sp_waited")

        def count(name, n, first, unit=1):
            return Count(sem(name), n, first, unit)

        x_loaded = count("x_loaded", 1, (-2, 0), 16)
        ln_step = count("ln_step", 2, (-2, 0))
        centred = count("centred", TB, (-1, 0))
        root_step = count("root_step", 3 * NEWTON + 3, (-2, 0))
        xn_made = count("xn_made", 1, (-2, 0))
        xn_turned = count("xn_turned", 2, (-1, 0))
        xf_stored = count("xf_stored", 2, (-1, 0))
        q_made = count("q_made", 2, (-1, 0))
        q_taken = count("q_taken", 2, (-1, 0))
        q_low = count("q_low", 2, (-1, 0))
        k_made = count("k_made", 2, (-1, 0))
        k_high = count("k_high", 2, (-1, 0))
        k_low = count("k_low", 2, (-1, 0))
        k_taken = count("k_taken", 2, (-1, 0))
        split_stored = [count(f"split_stored{c}", 4, (-1, 0), 16) for c in range(CH)]
        stack_loaded = [count(f"stack_loaded{g}", 6, (0 if g == 3 else -1, 0), 16) for g in range(NG)]
        pairs_summed = count("pairs_summed", 1, (-1, 0))
        pairs_taken = count("pairs_taken", 1, (-1, 0))
        band_turned = count("band_turned", 1, (-1, 0))
        band_taken = count("band_taken", 1, (-1, 0))
        v_made = count("v_made", 2, (-1, 0))
        v_taken = count("v_taken", 2, (-1, 0))
        v_own_made = count("v_own_made", 2, (-1, 0))
        v_shifted = count("v_shifted", 3, (-1, 0), 16)
        dx_made = count("dx_made", 2, (-1, 0))
        x_halved = count("x_halved", 2, (-1, 0))
        x_high_made = count("x_high_made", 2, (-1, 0))
        xk_high_made = count("xk_high_made", 2, (-1, 0))
        x_rested = count("x_rested", 2, (-1, 0))
        xk_halved = count("xk_halved", 2, (-1, 0))
        xk_rested = count("xk_rested", 2, (-1, 0))
        mixed = count("mixed", 4, (-1, 0))
        ffn_k_made = count("ffn_k_made", 2, (-1, 0))
        relu_made = count("relu_made", 2, (-1, 0))
        ffn_k_taken = count("ffn_k_taken", 2, (-1, 0))
        gate_made = count("gate_made", 2, (-1, 0))
        gate_taken = count("gate_taken", 2, (-1, 0))
        ffn_v_made = count("ffn_v_made", 2, (-1, 1))
        ffn_v_taken = count("ffn_v_taken", 2, (-1, 1))
        ffn_added = count("ffn_added", 2, (-1, 1))
        residual_copied = count("residual_copied", 2, (-1, 0))
        max_scored = count("max_scored", 64, (-1, 40))
        max_taken = count("max_taken", 64, (-1, 40))
        beside_made = count("beside_made", 3, (-1, 0))
        m_rounded = count("m_rounded", 4, (-1, 3))
        band_shifted = count("band_shifted", 4, (-1, 3))
        band_exped = count("band_exped", 4, (-1, 3))
        m_turned = count("m_turned", 4, (-1, 3))
        m_copied = count("m_copied", 4, (-1, 3))
        m_row = [count(f"m_row{g}", 1, (-1 if g == 0 else 0, 0), 16) for g in range(NG)]
        scored = count("scored", 40, (0, 0))
        probs_made = count("probs_made", 40, (0, 0))
        probs_masked = count("probs_masked", 32, (0, 0))
        o_added = count("o_added", 4, (0, 1))
        o_taken = count("o_taken", 4, (0, 2))
        band_step = count("band_step", 12, (0, 3))
        band_values = count("band_values", 4, (0, 1))
        heads_turned = count("heads_turned", 4, (0, 2))
        heads_taken = count("heads_taken", 4, (0, 2))
        head_step = count("head_step", 8, (0, 4))
        y_made = count("y_made", 4, (0, 2))
        y_turned = count("y_turned", 2, (1, 0))
        yT_stored = count("yT_stored", 2, (1, 0))
        o_made = count("o_made", 2, (1, 0))
        summed = count("summed", 2, (1, 0))
        out_stored = [count(f"out_stored{j}", 1, (1, 0), 16) for j in range(2)]

        last_read = dict(heads=heads_taken, ffn_v=ffn_v_taken, xf=xf_stored, q=q_taken, m=m_copied, k=k_high,
                         pairs=pairs_taken, band=band_taken, yT=yT_stored, v=v_taken, o=summed,
                         ffn_k=ffn_k_taken, gate=gate_taken)

        def spare_free(job, it):
            n, at, bank = job - 1, it, JOBS[job][4]
            while True:
                if n < 0:
                    n, at = n + len(JOBS), at - 1
                what, _, ahead, pos, b, _ = JOBS[n]
                if b == bank and (at.offset < -1 or (at + ahead).real(BATCHES)):
                    return last_read[what].after(at, pos)
                n -= 1

        def iterations(eng, body):
            for b in (-2, -1, 0):
                body(Batch(b))
            with eng.Fori(0, 3) as i:
                body(Batch(1, i))
                body(Batch(2, i))
            for b in (7, 8):
                body(Batch(b))

        def has_ln(it):
            return it.register is not None or it.offset <= 6

        def max_target(it, s):
            return (it, s + LEAD) if s + LEAD < STEPS else (it + 1, s + LEAD - STEPS)

        def max_back(n):
            back = 1
            while MAX_BANK[n - back] != MAX_BANK[n]:
                back += 1
            return back

        SETTLE = {1: (0, 1), 3: (0, 2), 5: (0, 3), 7: (1, 0)}
        TAIL = {0: (-1, 2), 2: (-1, 3), 4: (0, 0), 6: (0, 1)}
        TAKE = (5, 21, 38, 51)
        BAND = {1: (-1, 3), 3: (0, 0), 5: (0, 1), 7: (0, 2)}

        w_whole = [probs[0][:, n, 640:640 + CH * E].rearrange("p (c n) -> p c n", n=E) for n in range(3)]

        block = ctx.enter_context(nc.Block())

        @block.sync
        def _(sp):
            def load_weights():
                for n, (src, dst) in enumerate(((W_q, w_whole[0]), (W_k, w_whole[1]), (W_v, w_v), (W_o, w_o))):
                    sp.dma_start(dst[:, :, :], src.rearrange("(c p) n -> p c n", p=P)).then_inc(weights_in[n], 16)
                for n, src in enumerate((W_r, W_fk, W_fv)):
                    sp.dma_start(probs[0][:, n, 0:CH * E].rearrange("p (c n) -> p c n", c=CH),
                                 src.rearrange("(c p) n -> p c n", p=P)).then_inc(weights_in[4], 16)

            def load_stack(it, g):
                c, half = g // 2, g % 2
                q_src = split_q[c][half * P:(half + 1) * P, :]
                k_src = split_k[c][half * P:(half + 1) * P, :]
                sp.wait_ge(*split_stored[c].after(it, 3))
                sp.sem_inc(sp_waited, 1)
                if it.register is not None or it.offset >= 0:
                    sp.wait_ge(*scored.after(it, 10 * g + 9))
                both = "(h r) t -> r h t"
                sp.dma_start(q_stack[g][0:32, :, :], q_src.rearrange(both, r=32)).then_inc(stack_loaded[g].sem, 16)
                sp.dma_start(k_stack[g][0:32, :, :], k_src.rearrange(both, r=32)).then_inc(stack_loaded[g].sem, 16)
                sp.dma_start(k_stack[g][32:64, :, :], k_src.rearrange(both, r=32)).then_inc(stack_loaded[g].sem, 16)
                halves = q_src.rearrange("(h l e) t -> l e h t", l=2, e=HD)
                sp.dma_start(q_stack[g][32:48, :, :], halves[1]).then_inc(stack_loaded[g].sem, 16)
                sp.dma_start(q_stack[g][48:64, :, :], halves[0]).then_inc(stack_loaded[g].sem, 16)
                sp.dma_start(q_stack[g][64:65, :, :], q_stack[g][65:66, :, :]).then_inc(stack_loaded[g].sem, 16)

            def store_split(it, c):
                for n, (src, dst, half, ready) in enumerate((
                        (qh, split_q, 0, q_taken), (ql, split_q, 1, q_low),
                        (kh, split_k, 0, k_high), (kl, split_k, 1, k_low))):
                    if n == 0 and (it.register is not None or it.offset >= 0):
                        for g in (2 * c, 2 * c + 1):
                            sp.wait_ge(*stack_loaded[g].after(it if g == 3 else it - 1, 5))
                            sp.sem_inc(sp_waited, 1)
                    sp.wait_ge(*ready.after(it, c))
                    sp.dma_start(dst[c].rearrange("(h l e) t -> h l e t", l=2, e=HD)[:, half, :, :],
                                 src[:, c, :]).then_inc(split_stored[c].sem, 16)

            def body(it):
                nxt, late = it + 1, it - 1
                if it.real(BATCHES):
                    load_stack(late, 3)
                if has_ln(it):
                    if it.register is not None or it.offset > -2:
                        sp.wait_ge(*ln_step.after(late, 0))
                        sp.sem_inc(sp_waited, 1)
                    if it.register is not None or it.offset >= 0:
                        sp.wait_ge(*residual_copied.after(late, 1))
                    ahead = it + 2
                    where = ahead.offset if it.register is None else ahead.index() % BATCHES
                    sp.dma_start(x_nat[it.parity][:, :, :], x_rows[bass.ds(where, 1)].rearrange("o p t e -> p (o t) e")
                                 if it.register is not None else x_rows[where]).then_inc(x_loaded.sem, 16)
                if it.is_first(-2):
                    load_weights()
                if it.is_first(-1):
                    sp.wait_ge(zeros_ready, 2 * NG)
                if nxt.real(BATCHES):
                    store_split(it, 0)
                    load_stack(it, 0)
                    store_split(it, 1)
                    load_stack(it, 1)
                if late.real(BATCHES):
                    for j in range(2):
                        sp.wait_ge(*summed.after(it, j))
                        at = late.index()
                        dst = (out_rows[bass.ds(at, 1)].rearrange("o p t e -> p (o t) e")
                               if it.register is not None else out_rows[at])
                        sp.dma_start(dst[:, 2 * j:2 * j + 2, :], w_sum[late.parity][:, 2 * j:2 * j + 2, :]).then_inc(out_stored[j].sem, 16)
                if nxt.real(BATCHES):
                    sp.wait_ge(*v_taken.after(it, 1))
                    sp.sem_inc(sp_waited, 1)
                    sp.wait_ge(*band_values.after(it, 0))
                    prev = v_prev[nxt.parity]
                    sp.dma_start(prev[1:113, :, :], v_next[0:112, :, :]).then_inc(v_shifted.sem, 16)
                    sp.dma_start(prev[113:128, :, :], v_next[112:127, :, :]).then_inc(v_shifted.sem, 16)
                    sp.dma_start(prev[0:1, 1:TB, :], v_next[127:128, 0:TB - 1, :]).then_inc(v_shifted.sem, 16)
                    load_stack(it, 2)

            iterations(sp, body)
            for j in range(2):
                sp.wait_ge(*out_stored[j].after(Batch(BATCHES), 0))

        @block.gpsimd
        def _(pool):
            nc.gpsimd.memset(ident[:, :], 0.0).then_inc(consts_ready, 1)
            nc.gpsimd.memset(head_ones[:, :], 1.0).then_inc(consts_ready, 1)
            nc.gpsimd.memset(key_mask[:, :], 0.0).then_inc(consts_ready, 1)
            pool.wait_ge(consts_ready, 3)
            nc.gpsimd.affine_select(out=ident[:, :], in_=ident[:, :], compare_op=ALU.not_equal, fill=1.0,
                                    base=0, pattern=[[-1, P]], channel_multiplier=1).then_inc(consts_ready, 1)
            nc.gpsimd.affine_select(out=head_ones[:, :], in_=head_ones[:, :], compare_op=ALU.is_ge, fill=0.0,
                                    base=0, pattern=[[-HD, 32]], channel_multiplier=1).then_inc(consts_ready, 1)
            nc.gpsimd.affine_select(out=key_mask[:, :], in_=key_mask[:, :], compare_op=ALU.is_ge, fill=MASKED,
                                    base=SEQ - P - 2, pattern=[[-1, SEQ]], channel_multiplier=1).then_inc(consts_ready, 1)
            pool.wait_ge(consts_ready, 6)
            nc.gpsimd.affine_select(out=head_ones[:, :], in_=head_ones[:, :], compare_op=ALU.is_ge, fill=0.0,
                                    base=HD - 1, pattern=[[HD, 32]], channel_multiplier=-1).then_inc(consts_ready, 1)
            nc.gpsimd.tensor_copy(ident16[:, :], ident[:, :]).then_inc(consts_ready, 1)
            nc.gpsimd.memset(one[:, :], 1.0).then_inc(consts_ready, 1)
            nc.gpsimd.memset(xf[:, :, 0:1], 0.0).then_inc(consts_ready, 1)
            nc.gpsimd.memset(band_prod[:, 1, :, 0:1], 0.0).then_inc(consts_ready, 1)
            for i in range(2):
                nc.gpsimd.memset(v_prev[i][0:1, 0, :], 0.0).then_inc(consts_ready, 1)
                nc.gpsimd.memset(v0[i][:, :, :, HD:2 * HD], 1.0).then_inc(consts_ready, 1)
            pool.wait_ge(consts_ready, 15)
            for g in range(NG):
                nc.gpsimd.memset(q_stack[g][64:128, :, :].bitcast(F32), 0.0).then_inc(zeros_ready, 1)
                nc.gpsimd.memset(k_stack[g][64:128, :, :].bitcast(F32), TWO_UNITS).then_inc(zeros_ready, 1)
            pool.wait_ge(zeros_ready, 2 * NG)

            def split_q_low(it, c):
                pool.wait_ge(*q_taken.after(it, c))
                pool.wait_ge(*split_stored[c].after(it - 1, 3))
                nc.gpsimd.tensor_tensor(ql[:, c, :], qf[:, c, :], qh[:, c, :], ALU.subtract).then_inc(q_low.sem, 1)

            def split_k_low(it, c):
                pool.wait_ge(*k_high.after(it, c))
                pool.wait_ge(*split_stored[c].after(it - 1, 3))
                nc.gpsimd.tensor_tensor(kl[:, c, :], kf[:, c, :], kh[:, c, :], ALU.subtract).then_inc(k_low.sem, 1)

            def body(it):
                nxt = it + 1
                for s in range(STEPS):
                    if s == 0 and nxt.real(BATCHES):
                        for c in range(CH):
                            pool.wait_ge(*x_high_made.after(it, c))
                            nc.gpsimd.tensor_tensor(x_low[:, c, :], xf[:, c, 1:SEQ + 1], x_high[:, c, :].bitcast(F32),
                                                    ALU.subtract).then_inc(x_rested.sem, 1)
                        for c in range(CH):
                            pool.wait_ge(*xf_stored.after(it, c))
                            if c == 0:
                                pool.wait_ge(*ffn_k_made.after(it - 1, 1))
                            nc.gpsimd.tensor_tensor(dx[:, c, :], xf[:, c, 0:SEQ], xf[:, c, 1:SEQ + 1],
                                                    ALU.subtract).then_inc(dx_made.sem, 1)
                    if s == 1 and it.real(BATCHES):
                        pool.wait_ge(*ffn_v_taken.after(it, 0))
                        pool.wait_ge(*residual_copied.after(it - 1, 1))
                        w = w_sum[it.parity][:, 2:4, :]
                        nc.gpsimd.tensor_tensor(w, w, gate[:, 2:4, :], ALU.add).then_inc(ffn_added.sem, 1)
                    if s in (2, 3) and nxt.real(BATCHES):
                        split_k_low(it, s - 2)
                    if s == 2 and nxt.real(BATCHES):
                        split_q_low(it, 1)
                    if it.real(BATCHES):
                        g, i0 = s // 2, 2 * (s % 2)
                        pr = probs[g % 2][:, i0:i0 + 2, :]
                        for j, f in ((0, 2), (1, 3), (3, 3), (2, 4)):
                            pool.wait_ge(*probs_made.after(it, 5 * s + f))
                            pool.sem_inc(pool_waited, 1)
                            width = P if j == TB - 1 else P + 1
                            part = pr[:, :, KEY_AT[j]:KEY_AT[j] + width]
                            nc.gpsimd.affine_select(out=part, in_=part, compare_op=ALU.is_ge, fill=0.0, base=-2,
                                                    pattern=[[0, 2], [1, width]],
                                                    channel_multiplier=-1).then_inc(probs_masked.sem, 1)
                    if s == 1 and nxt.real(BATCHES):
                        split_q_low(it, 0)
                    if s in (4, 6) and nxt.real(BATCHES):
                        j = (s - 4) // 2
                        pool.wait_ge(*v_taken.after(it, j))
                        if j == 0:
                            pool.wait_ge(*band_values.after(it, 0))
                        nc.gpsimd.tensor_tensor(
                            v_own[nxt.parity][:, 2 * j:2 * j + 2, :].rearrange("p t (h d) -> p t h d", d=HD),
                            v0[nxt.parity][:, 2 * j:2 * j + 2, :, 0:HD],
                            v_bias[:, 2, :].rearrange("p (h d) -> p h d", d=HD).unsqueeze(1).to_broadcast([P, 2, HEADS, HD]),
                            ALU.add).then_inc(v_own_made.sem, 1)
                    if s == 4 and nxt.real(BATCHES):
                        for c in range(CH):
                            pool.wait_ge(*xk_high_made.after(it, c))
                            nc.gpsimd.tensor_tensor(x_low[:, c, :], xk[:, c, :], x_high[:, c, :].bitcast(F32),
                                                    ALU.subtract).then_inc(xk_rested.sem, 1)
                    if s in BAND and (it + BAND[s][0]).real(BATCHES):
                        at, g = it + BAND[s][0], BAND[s][1]
                        pos = g + 1
                        e_own = band_exp[g][:, 0].rearrange("p h t -> p t h")
                        e_prev = band_exp[g][:, 1].rearrange("p h t -> p t h")
                        hs = slice(GROUP * g * HD, GROUP * (g + 1) * HD)
                        own = v_own[at.parity][:, :, hs].rearrange("p t (h d) -> p t h d", d=HD)
                        prev = v_prev[at.parity][:, :, hs].rearrange("p t (h d) -> p t h d", d=HD)
                        wide = [P, TB, GROUP, HD]
                        pool.wait_ge(*band_exped.after(at, g - 1))
                        pool.wait_ge(*v_own_made.after(at - 1, 1))
                        pool.wait_ge(*v_shifted.after(at - 1, 2))
                        pool.wait_ge(*heads_taken.after(at, g + 1))
                        nc.gpsimd.tensor_tensor(band_sum[:, :, :], band_exp[g][:, 0], band_exp[g][:, 1],
                                                ALU.add).then_inc(band_step.sem, 1)
                        nc.gpsimd.tensor_tensor(band_a[:, :, :, :], own, e_own.unsqueeze(3).to_broadcast(wide),
                                                ALU.mult).then_inc(band_step.sem, 1)
                        nc.gpsimd.tensor_tensor(band_b[:, :, :, :], prev, e_prev.unsqueeze(3).to_broadcast(wide),
                                                ALU.mult).then_inc(band_step.sem, 1)
                        pool.wait_ge(*band_step.after(at, 3 * pos + 2))
                        nc.gpsimd.tensor_tensor(band_v[:, :, :, :], band_a[:, :, :, :], band_b[:, :, :, :],
                                                ALU.add).then_inc(band_values.sem, 1)
                    if s in (5, 6) and nxt.real(BATCHES):
                        j = s - 5
                        pool.wait_ge(*out_stored[j].after(it, 0))
                        pool.wait_ge(*x_loaded.after(it - 1, 0))
                        w = w_sum[nxt.parity][:, 2 * j:2 * j + 2, :]
                        nc.gpsimd.tensor_tensor(w, x_nat[nxt.parity][:, 2 * j:2 * j + 2, :],
                                                b_o_all[:, :].unsqueeze(1).to_broadcast([P, 2, E]),
                                                ALU.add).then_inc(residual_copied.sem, 1)
                    if s == 7 and nxt.real(BATCHES):
                        pool.wait_ge(*ffn_v_taken.after(it, 1))
                        pool.wait_ge(*residual_copied.after(it, 0))
                        w = w_sum[nxt.parity][:, 0:2, :]
                        nc.gpsimd.tensor_tensor(w, w, gate[:, 0:2, :], ALU.add).then_inc(ffn_added.sem, 1)

            iterations(pool, body)

        @block.scalar
        def _(act):
            for part, src in ((rows[0:1, 0, :], b_q), (b_k_row[:, :], b_k), (mu_rows[0:1, 0, :], mu_r),
                              (mu_rows[0:1, 1, :], mu_k)):
                act.dma_start(part, src.rearrange("(o n) -> o n", o=1)).then_inc(rows_in, 16)
            act.dma_start(rel_row[:, :, :], rel_k[0:3, :].rearrange("(o r) d -> o r d", o=1)).then_inc(rows_in, 16)
            act.dma_start(rel_v_all[:, :, :],
                           rel_v[0:3, :].rearrange("(o r) d -> o r d", o=1).to_broadcast([P, 3, HD])).then_inc(rows_in, 16)
            act.dma_start(b_v_all[:, :], b_v.rearrange("(o n) -> o n", o=1).to_broadcast([P, E])).then_inc(rows_in, 16)
            act.dma_start(b_o_all[:, :], b_o.rearrange("(o n) -> o n", o=1).to_broadcast([P, E])).then_inc(rows_in, 16)

            def take_weights():
                for n, dst in enumerate((w_rT, w_whole[2], w_fvT)):
                    act.wait_ge(turned_weights, n + 1)
                    nc.scalar.activation(dst[:, :, :], bank[3 + n][:, :].rearrange("p (c n) -> p c n", c=CH),
                                         ACT.Copy, scale=0.5 if dst is w_fvT else 1.0).then_inc(weights_taken, 1)

            def take_cols():
                act.wait_ge(cols_made, 1)
                nc.scalar.activation(cols[:, :, :], o_bank[:, 0:12].rearrange("p (a c) -> p a c", c=CH),
                                     ACT.Copy).then_inc(cols_taken, 1)
                act.wait_ge(cols_taken, 1)

            def take_gate(it, j):
                act.wait_ge(*gate_made.after(it, j))
                act.wait_ge(*ffn_added.after(it if j else it - 1, 1 - j))
                nc.scalar.activation(gate[:, 2 * j:2 * j + 2, :],
                                     spare[BANK_OF["gate", j]][:, :].rearrange("p (t n) -> p t n", t=2),
                                     ACT.Tanh, scale=0.5).then_inc(gate_taken.sem, 1)

            def body(it):
                nxt, late = it + 1, it - 1
                for s in range(STEPS):
                    for k in range(SLOTS):
                        n = SLOTS * s + k
                        if k == 0 and s in TAIL and (it + TAIL[s][0]).real(BATCHES):
                            at, g = it + TAIL[s][0], TAIL[s][1]
                            act.wait_ge(*o_added.after(at, g + 1))
                            act.wait_ge(*heads_turned.after(at, g + 1))
                            nc.scalar.activation(oT[:, :], o_bank[:, :], ACT.Copy).then_inc(o_taken.sem, 1)
                        if n == 5 and it.is_first(-1):
                            take_cols()
                        if n == 8 and it.is_first(-1):
                            take_weights()
                        if n in (1, 4) and nxt.real(BATCHES):
                            c = n // 4
                            act.wait_ge(*xn_turned.after(it, c))
                            act.wait_ge(*v_made.after(late, 1))
                            act.wait_ge(*mixed.after(late, 3))
                            nc.scalar.activation(xf[:, c, 1:SEQ + 1], spare[BANK_OF["xf", c]][:, :],
                                                 ACT.Copy).then_inc(xf_stored.sem, 1)
                        if n in (3, 6, 35, 37) and nxt.real(BATCHES):
                            c = int(n in (6, 37))
                            halved, done = (x_halved, x_high_made) if n < 8 else (xk_halved, xk_high_made)
                            act.wait_ge(*halved.after(it, c))
                            act.wait_ge(*(ffn_k_made.after(late, 1) if n < 8 else k_made.after(it, 1)))
                            nc.scalar.activation(x_high[:, c, :], cut[:, :],
                                                 ACT.Copy).then_inc(done.sem, 1)
                        if s in SETTLE and n == {1: 12, 3: 26, 5: 42, 7: 59}[s] and (it + SETTLE[s][0]).real(BATCHES):
                            at, g = it + SETTLE[s][0], SETTLE[s][1]
                            act.wait_ge(*m_turned.after(at, g - 1))
                            before = (at, g - 1) if g else (at - 1, 3)
                            act.wait_ge(*m_row[before[1]].after(before[0] - (before[1] == 0), 0))
                            nc.scalar.activation(mT[:, :], spare[BANK_OF["m", g]][0:HEADS, 0:P // 2].bitcast(F16),
                                                 ACT.Copy).then_inc(m_copied.sem, 1)
                            act.wait_ge(*m_copied.after(at, g - 1))
                            act.dma_start(q_stack[g][64:65, :, :].rearrange("p h (t q) -> p (h t) q", q=P),
                                          mT[:, :]).then_inc(m_row[g].sem, 16)
                        if n in (12, 20) and nxt.real(BATCHES):
                            c = n // 20
                            src = spare[BANK_OF["q", c]]
                            act.wait_ge(*q_made.after(it, c))
                            act.wait_ge(*k_taken.after(late, c))
                            act.wait_ge(*split_stored[c].after(late, 3))
                            nc.scalar.activation(qf[:, c, :], src[:, :], ACT.Identity, bias=cols[:, 0, c:c + 1])
                            nc.scalar.activation(qh[:, c, :], src[:, :], ACT.Identity,
                                                 bias=cols[:, 0, c:c + 1]).then_inc(q_taken.sem, 1)
                        if n in (16, 24) and nxt.real(BATCHES):
                            c = n // 24
                            src = spare[BANK_OF["k", c]]
                            act.wait_ge(*k_made.after(it, c))
                            act.wait_ge(*k_taken.after(late, c))
                            act.wait_ge(*split_stored[c].after(late, 3))
                            nc.scalar.activation(kf[:, c, :], src[:, :], ACT.Identity, bias=cols[:, 1, c:c + 1])
                            nc.scalar.activation(kh[:, c, :], src[:, :], ACT.Identity,
                                                 bias=cols[:, 1, c:c + 1]).then_inc(k_high.sem, 1)
                        if n == 30 and nxt.real(BATCHES):
                            act.wait_ge(*pairs_summed.after(it, 0))
                            act.wait_ge(*xn_turned.after(it, 1))
                            nc.scalar.activation(pair_rows[:, :], spare[BANK_OF["pairs", 0]][:, :],
                                                 ACT.Copy).then_inc(pairs_taken.sem, 1)
                        if n == 32 and nxt.real(BATCHES):
                            act.wait_ge(*band_turned.after(it, 0))
                            nc.scalar.activation(band[nxt.parity][:, :, :, :].rearrange("p t a (c h) -> p (t a c) h", h=8),
                                                 spare[BANK_OF["band", 0]][:, :].rearrange("p (g w) -> p g w", w=32)[:, :, 0:8],
                                                 ACT.Copy).then_inc(band_taken.sem, 1)
                        if s in SETTLE and (it + SETTLE[s][0]).real(BATCHES):
                            at, g = it + SETTLE[s][0], SETTLE[s][1]
                            if k == 3:
                                act.wait_ge(*band_shifted.after(at, g - 1))
                                act.wait_ge(*band_values.after(at - 1, g + 1))
                                nc.scalar.activation(band_exp[g][:, :, :, :], band_arg[g][:, :, :, :], ACT.Exp,
                                                     scale=SCALE).then_inc(band_exped.sem, 1)
                        if n in (34, 36) and late.real(BATCHES):
                            c = (n - 34) // 2
                            act.wait_ge(*y_turned.after(it, c))
                            if nxt.real(BATCHES):
                                act.wait_ge(*band_taken.after(it, 0))
                            nc.scalar.activation(yT[:, c, :], spare[BANK_OF["yT", c]][:, :],
                                                 ACT.Copy).then_inc(yT_stored.sem, 1)
                        if n in (48, 54) and nxt.real(BATCHES):
                            c = (n - 48) // 6
                            act.wait_ge(*ffn_k_made.after(it, c))
                            act.wait_ge(*ffn_k_taken.after(late, c))
                            nc.scalar.activation(ffn_act[:, c, :], spare[BANK_OF["ffn_k", c]][:, :],
                                                 ACT.Relu).then_inc(relu_made.sem, 1)
                        if n in range(44, 49) and has_ln(it) and not it.is_first(-2):
                            if n < 44 + TB:
                                t = n - 44
                                if t == 0:
                                    act.wait_ge(*ln_step.after(it, 1))
                                    if nxt.real(BATCHES):
                                        act.wait_ge(*band_turned.after(it, 0))
                                    if late.real(BATCHES):
                                        act.wait_ge(*o_made.after(it, 1))
                                nc.scalar.activation(xn[:, t, :], x_nat[it.parity][:, t, :], ACT.Identity,
                                                     bias=neg_mean[:, t:t + 1]).then_inc(centred.sem, 1)
                            if n > 44:
                                t = n - 45
                                act.wait_ge(*centred.after(it, t))
                                last = nc.scalar.activation(xn[:, t, :], xn[:, t, :], ACT.Copy, scale=rstd[:, t:t + 1])
                                if t == TB - 1:
                                    last.then_inc(xn_made.sem, 1)
                        if n == 57 and nxt.real(BATCHES):
                            take_gate(it, 0)
                        if k in FILL_SLOT and it.real(BATCHES):
                            f, g, i0 = FILL_SLOT[k], s // 2, 2 * (s % 2)
                            b, parts = (5 * s + f) % 2, FILLS[f]
                            act.wait_ge(*scored.after(it, 5 * s + f))
                            if f == 0 and s % 2 == 0:
                                act.wait_ge(*o_added.after(it, g - 1))
                            if f == 4:
                                dst = probs[g % 2][:, i0:i0 + 2, KEY_AT[2]:KEY_AT[2] + 256]
                                src = fill_bank[b][:, :].rearrange("p (h w) -> p h w", h=2)
                            else:
                                h, j, _ = parts[-1]
                                dst = probs[g % 2][:, i0 + h, KEY_AT[j]:KEY_AT[j] + 512]
                                src = fill_bank[b][:, :]
                            nc.scalar.activation(dst, src, ACT.Exp, scale=SCALE).then_inc(probs_made.sem, 1)
                if nxt.real(BATCHES):
                    take_gate(it, 1)

            iterations(act, body)

        @block.vector
        def _(dve):
            def make_rows():
                dve.wait_ge(rows_in, 8 * 16)
                per_head = "p (h d) -> p h d"
                first_rel = rel_row[:, 0, :].unsqueeze(1).to_broadcast([1, HEADS, HD])
                nc.vector.tensor_tensor(rows[0:1, 1, :].rearrange(per_head, d=HD),
                                        b_k_row[:, :].rearrange(per_head, d=HD), first_rel, ALU.add)
                for n, r in ((2, 2), (3, 1)):
                    nc.vector.tensor_tensor(rows[0:1, n, :].rearrange(per_head, d=HD),
                                            rel_row[:, r, :].unsqueeze(1).to_broadcast([1, HEADS, HD]), first_rel,
                                            ALU.subtract)
                nc.vector.tensor_scalar(rows[0:1, 4:6, :], mu_rows[:, :, :], -1.0, 1.0, ALU.mult,
                                        ALU.add).then_inc(rows_ready, 1)
            def add_value_biases():
                per_head = "p (h d) -> p h d"
                for r in range(3):
                    wide = lambda n: rel_v_all[:, n, :].unsqueeze(1).to_broadcast([P, HEADS, HD])
                    first = wide(2) if r == 2 else b_v_all[:, :].rearrange(per_head, d=HD)
                    nc.vector.tensor_tensor(v_bias[:, r, :].rearrange(per_head, d=HD), first, wide(r % 2),
                                            ALU.subtract if r == 2 else ALU.add).then_inc(vconsts_ready, 1)

            def halve_weights(n):
                whole, high, low = w_whole[n], w_high[n], w_low[n]
                if n > 0:
                    dve.wait_ge(*x_high_made.after(Batch(-1), 1))
                part = cut[:, :].rearrange("p (c n) -> p c n", c=CH)
                nc.vector.tensor_scalar(part.bitcast(I32), whole[:, :, :].bitcast(I32), HIGH_BITS, None,
                                        ALU.bitwise_and).then_inc(w_halved, 1)
                dve.wait_ge(w_halved, 3 * n + 1)
                nc.vector.tensor_copy(high[:, :, :], part).then_inc(w_halved, 1)
                dve.wait_ge(w_halved, 3 * n + 2)
                nc.vector.tensor_tensor(low[:, :, :], whole[:, :, :], high[:, :, :].bitcast(F32),
                                        ALU.subtract).then_inc(w_halved, 1)

            def halve_x(it, c, src, made, done):
                dve.wait_ge(*(x_high_made if made is xf_stored else xk_high_made).after(it, c - 1))
                if made is xf_stored:
                    dve.wait_ge(*xf_stored.after(it, c))
                else:
                    dve.wait_ge(*mixed.after(it, 2 + c))
                nc.vector.tensor_scalar(cut[:, :].bitcast(I32), src.bitcast(I32), HIGH_BITS, None,
                                        ALU.bitwise_and).then_inc(done.sem, 1)

            def finish_setup():
                dve.wait_ge(vconsts_ready, 3)
                dve.wait_ge(consts_ready, 15)
                dve.wait_ge(cols_taken, 1)

            def take_heads(it, s):
                at, g = it + TAIL[s][0], TAIL[s][1]
                src = spare[BANK_OF["heads", g]][:, :].rearrange("p (t h d) -> p t h d", t=TB, h=GROUP)
                dve.wait_ge(*heads_turned.after(at, g + 2))
                dve.wait_ge(*band_values.after(at, g + 1))
                dve.wait_ge(*y_made.after(at, g + 1))
                nc.vector.tensor_tensor(denom[:, :, :], src[:, :, :, HD],
                                        band_sum[:, :, :].rearrange("p h t -> p t h"),
                                        ALU.add).then_inc(head_step.sem, 1)
                nc.vector.tensor_tensor(num[:, :, :, :], src[:, :, :, 0:HD], band_v[:, :, :, :],
                                        ALU.add).then_inc(heads_taken.sem, 1)

            def invert(it, s):
                at, g = it + TAIL[s][0], TAIL[s][1]
                dve.wait_ge(*head_step.after(at, 2 * g + 4))
                nc.vector.reciprocal(inv[:, :, :], denom[:, :, :]).then_inc(head_step.sem, 1)

            def normalise(it, s):
                at, g = it + TAIL[s][0], TAIL[s][1]
                dve.wait_ge(*heads_taken.after(at, g + 2))
                dve.wait_ge(*head_step.after(at, 2 * g + 5))
                nc.vector.tensor_tensor(y[:, :, GROUP * g * HD:GROUP * (g + 1) * HD].rearrange("p t (h d) -> p t h d", d=HD),
                                        num[:, :, :, :], inv[:, :, :].unsqueeze(3).to_broadcast([P, TB, GROUP, HD]),
                                        ALU.mult).then_inc(y_made.sem, 1)

            def root_step_at(it, n):
                bits = mybir.dt.int32
                dve.wait_ge(*(root_step.after(it, n - 1) if n else ln_aggr.after(it, 0)))
                if n == 0:
                    nc.vector.tensor_scalar(neg_mean[:, :], mean_var[:, :, 0], -1.0, None, ALU.mult)
                    made = nc.vector.tensor_scalar(var_eps[:, :], mean_var[:, :, 1], EPS, None, ALU.add)
                elif n == 1:
                    made = nc.vector.tensor_scalar(root_a[:, :].bitcast(bits), var_eps[:, :].bitcast(bits), 1, None,
                                                   ALU.logical_shift_right)
                elif n == 2:
                    made = nc.vector.tensor_scalar(rstd[:, :].bitcast(bits), root_a[:, :].bitcast(bits), -1,
                                                   ROOT_GUESS, ALU.mult, ALU.add)
                elif n % 3 == 0:
                    made = nc.vector.scalar_tensor_tensor(root_a[:, :], rstd[:, :], -0.5, rstd[:, :], ALU.mult, ALU.mult)
                elif n % 3 == 1:
                    made = nc.vector.tensor_tensor(root_b[:, :], root_a[:, :], var_eps[:, :], ALU.mult)
                else:
                    made = nc.vector.scalar_tensor_tensor(rstd[:, :], root_b[:, :], 1.5, rstd[:, :], ALU.add, ALU.mult)
                made.then_inc(root_step.sem, 1)
                if n == 3 * NEWTON + 2:
                    dve.wait_ge(*root_step.after(it, n))
                    dve.sem_inc(ln_step.sem, 1)

            def settle_max(it, s):
                at, g = it + SETTLE[s][0], SETTLE[s][1]
                apart = beside[:, :, GROUP * g:GROUP * (g + 1)].rearrange("p t h -> p h t")
                dve.wait_ge(*max_taken.after(at, 8 * (2 * g + 1 - LEAD) + 7))
                if g == 0:
                    dve.wait_ge(*beside_made.after(at - 1, 2))
                nc.vector.scalar_tensor_tensor(m16[g][:, :, :], mx[g][:, :, :], -1.0 / M_UNIT, apart,
                                               ALU.mult, ALU.min).then_inc(m_rounded.sem, 1)

            def prepare_band(it, n):
                scores = band[(it + 1).parity]
                if n == 0:
                    dve.wait_ge(*band_taken.after(it, 0))
                    made = nc.vector.memset(scores[0:1, 0, 1, :], MASKED)
                elif n == 1:
                    dve.wait_ge(*beside_made.after(it, 0))
                    made = nc.vector.tensor_tensor(beside[:, :, :], scores[:, :, 0, :], scores[:, :, 1, :], ALU.max)
                else:
                    dve.wait_ge(*beside_made.after(it, 1))
                    made = nc.vector.tensor_scalar(beside[:, :, :], beside[:, :, :], -1.0 / M_UNIT, None, ALU.mult)
                made.then_inc(beside_made.sem, 1)

            def shift_band(it, s):
                at, g = it + SETTLE[s][0], SETTLE[s][1]
                pair = band[at.parity][:, :, :, GROUP * g:GROUP * (g + 1)]
                dve.wait_ge(*m_rounded.after(at, g - 1))
                dve.wait_ge(*band_exped.after(at - 1, g - 1))
                for n in range(2):
                    last = nc.vector.scalar_tensor_tensor(band_arg[g][:, n], m16[g][:, :, :], M_UNIT,
                                                          pair[:, :, n, :].rearrange("p t h -> p h t"),
                                                          ALU.mult, ALU.add)
                last.then_inc(band_shifted.sem, 1)

            def body(it):
                nxt, late = it + 1, it - 1
                for s in range(STEPS):
                    for k in range(SLOTS):
                        n = SLOTS * s + k
                        if it.is_first(-1):
                            if n == 0:
                                make_rows()
                                dve.wait_ge(weights_in[0], 16)
                                halve_weights(0)
                            if n == 6:
                                dve.wait_ge(weights_in[1], 16)
                                halve_weights(1)
                            if n == 9:
                                add_value_biases()
                            if n == 12:
                                dve.wait_ge(weights_taken, 2)
                                halve_weights(2)
                            if n == 10:
                                finish_setup()
                        for part, lag in ((take_heads, 0), (invert, 1), (normalise, 2)):
                            begun = (n - lag) // SLOTS
                            if n - lag in TAKE and (it + TAIL[begun][0]).real(BATCHES):
                                part(it, begun)
                        if s in SETTLE and k < 2 and (it + SETTLE[s][0]).real(BATCHES):
                            (settle_max, shift_band)[k](it, s)
                        if n in (9, 62) and (it + n // 62).real(BATCHES):
                            at, j, pos = (it, 1, 0) if n == 9 else (nxt, 0, 1)
                            dve.wait_ge(*ffn_v_made.after(it, pos))
                            dve.wait_ge(*gate_taken.after(at - 1, j))
                            half = gate[:, 2 * j:2 * j + 2, :]
                            nc.vector.scalar_tensor_tensor(half, half, 1.0,
                                                           spare[BANK_OF["ffn_v", j]][:, :].rearrange("p (t n) -> p t n", t=2),
                                                           ALU.add, ALU.mult).then_inc(ffn_v_taken.sem, 1)
                        if n in (18, 19, 26, 27) and nxt.real(BATCHES):
                            c, part = (n - 18) // 8, (n - 18) % 8
                            if part == 0:
                                dve.wait_ge(*k_high.after(it, c))
                                dve.wait_ge(*q_taken.after(it, c))
                                dve.wait_ge(*pairs_summed.after(late, 0))
                                dve.wait_ge(*v_shifted.after(late, 2))
                                nc.vector.scalar_tensor_tensor(band_prod[:, 0, c, :], kf[:, c, :], cols[:, 2, c:c + 1],
                                                               qf[:, c, :], ALU.add, ALU.mult)
                            else:
                                nc.vector.scalar_tensor_tensor(band_prod[:, 1, c, 1:SEQ], kf[:, c, 0:SEQ - 1],
                                                               cols[:, 3, c:c + 1], qf[:, c, 1:SEQ],
                                                               ALU.add, ALU.mult).then_inc(k_taken.sem, 1)
                        if n in (2, 5) and nxt.real(BATCHES):
                            c = n // 5
                            halve_x(it, c, xf[:, c, 1:SEQ + 1], xf_stored, x_halved)
                        if n in (34, 35) and nxt.real(BATCHES):
                            c = n - 34
                            halve_x(it, c, xk[:, c, :], None, xk_halved)
                        if n in (13, 15, 28, 30) and nxt.real(BATCHES):
                            c = (13, 15, 28, 30).index(n) % 2
                            dst, row = (xr, 4) if n < 28 else (xk, 5)
                            dve.wait_ge(*dx_made.after(it, c))
                            if n >= 28:
                                dve.wait_ge(*mixed.after(it, c))
                            nc.vector.scalar_tensor_tensor(dst[:, c, :], dx[:, c, :], cols[:, row, c:c + 1],
                                                           xf[:, c, 1:SEQ + 1], ALU.mult,
                                                           ALU.add).then_inc(mixed.sem, 1)
                        if n in (31, 32, 46, 47) and nxt.real(BATCHES):
                            j, r = (n - 31) // 15, (n - 31) % 15
                            src = spare[BANK_OF["v", j]][:, :].rearrange("p (t h d) -> p t h d", t=2, h=HEADS)
                            if r == 0:
                                dve.wait_ge(*v_made.after(it, j))
                            if n == 31:
                                dve.wait_ge(*pairs_summed.after(it, 0))
                            ts = slice(2 * j, 2 * j + 2)
                            dst = (v0[nxt.parity][:, ts, :, 0:HD],
                                   v_next[:, ts, :].rearrange("p t (h d) -> p t h d", d=HD))[r]
                            bias = v_bias[:, r, :].rearrange("p (h d) -> p h d", d=HD).unsqueeze(1)
                            last = nc.vector.tensor_tensor(dst, src, bias.to_broadcast([P, 2, HEADS, HD]), ALU.add)
                            if r == 1:
                                last.then_inc(v_taken.sem, 1)
                        if n in (40, 44) and late.real(BATCHES):
                            j = (n - 40) // 4
                            dve.wait_ge(*o_made.after(it, j))
                            dve.wait_ge(*ffn_added.after(late, 0))
                            w = w_sum[late.parity][:, 2 * j:2 * j + 2, :]
                            nc.vector.tensor_tensor(w, w,
                                                    spare[BANK_OF["o", j]][:, :].rearrange("p (t n) -> p t n", t=2),
                                                    ALU.add).then_inc(summed.sem, 1)
                        if n == 44 and it.is_first(-2):
                            dve.wait_ge(*ln_step.after(it, 1))
                            for t in range(TB):
                                last = nc.vector.tensor_scalar(xn[:, t, :], x_nat[0][:, t, :], mean_var[:, t, 0:1],
                                                               rstd[:, t:t + 1], ALU.subtract, ALU.mult)
                            last.then_inc(xn_made.sem, 1)
                        if n in (49, 55) and nxt.real(BATCHES):
                            c = (n - 49) // 6
                            dve.wait_ge(*relu_made.after(it, c))
                            nc.vector.scalar_tensor_tensor(ffn_act[:, c, :], spare[BANK_OF["ffn_k", c]][:, :], 0.0,
                                                           ffn_act[:, c, :], ALU.max, ALU.mult).then_inc(ffn_k_taken.sem, 1)
                        if n in (10, 11, 12, 14) and has_ln(it):
                            t = (10, 11, 12, 14).index(n)
                            if t == 0:
                                dve.wait_ge(*x_loaded.after(it, 0))
                            last = nc.vector.bn_stats(stats[:, t, :], x_nat[it.parity][:, t, :])
                            if t == TB - 1:
                                last.then_inc(ln_step.sem, 1)
                        if n == 17 and has_ln(it):
                            dve.wait_ge(*xn_made.after(late, 0))
                            dve.wait_ge(*ln_step.after(it, 0))
                            dve.sem_inc(dve_waited, 1)
                            for t in range(TB):
                                last = nc.vector.bn_aggr(mean_var[:, t, :], stats[:, t, :])
                            last.then_inc(ln_aggr.sem, 1)
                        root_slot = 18 if it.is_first(-1) else 30
                        if n in range(root_slot, root_slot + 3 * NEWTON + 3) and has_ln(it):
                            root_step_at(it, n - root_slot)
                        if n in (51, 52, 53) and nxt.real(BATCHES):
                            prepare_band(it, n - 51)
                        at, pair = max_target(it, s)
                        if at.real(BATCHES):
                            g, i, qb = pair // 2, 2 * (pair % 2) + k // 4, TB - 1 - k % 4
                            width = P * (qb + 1)
                            dve.wait_ge(*max_scored.after(it, 8 * s + k))
                            dve.sem_inc(dve_waited, 1)
                            nc.vector.tensor_tensor_reduce(out=max_bank[MAX_BANK[n]][:, 0:width], in0=max_bank[MAX_BANK[n]][:, 0:width],
                                                           in1=key_mask[:, SEQ - width:SEQ], scale=1.0,
                                                           scalar=MASKED, op0=ALU.add, op1=ALU.max,
                                                           accum_out=mx[g][:, i, qb:qb + 1]).then_inc(max_taken.sem, 1)

            ln_aggr = count("ln_aggr", 1, (-2, 0))
            iterations(dve, body)

        @block.tensor
        def _(pe):
            def turn_weights():
                pe.wait_ge(weights_in[4], 3 * 16)
                pe.wait_ge(cols_taken, 1)
                for n in range(3):
                    for ci in range(CH):
                        for di in range(CH):
                            at = E * di + P * ci
                            last = nc.tensor.transpose(bank[3 + n][:, E * ci + P * di:E * ci + P * (di + 1)],
                                                       probs[0][:, n, at:at + P], ident[:, :])
                    last.then_inc(turned_weights, 1)

            def turn_rows():
                pe.wait_ge(rows_ready, 1)
                for r in range(6):
                    for c in range(CH):
                        last = nc.tensor.matmul(o_bank[:, CH * r + c:CH * r + c + 1], rows[0:1, r, P * c:P * (c + 1)],
                                                one[:, :], start=True, stop=True)
                last.then_inc(cols_made, 1)

            def wait_for_setup(n):
                if n == 0:
                    pe.wait_ge(consts_ready, 15)
                if n == 4:
                    turn_rows()
                if n == 9:
                    pe.wait_ge(w_halved, 3)
                if n == 13:
                    pe.wait_ge(w_halved, 6)
                if n == 7:
                    turn_weights()
                if n == 26:
                    pe.wait_ge(weights_in[2], 16)
                    pe.wait_ge(weights_in[3], 16)
                if n == 40:
                    pe.wait_ge(zeros_ready, 2 * NG)
                    pe.wait_ge(vconsts_ready, 3)
                if n == 46:
                    pe.wait_ge(w_halved, 9)
                    pe.wait_ge(weights_taken, 3)

            def spare_work(it, job, n):
                what, which, ahead, pos, b, parts = JOBS[job]
                of, late, dst = it + ahead, it - 1, spare[b]
                token_blocks = dict(v=(w_v, xf, 1, v_made), o=(w_o, yT, 0, o_made), gate=(w_rT, xr, 0, gate_made),
                                    ffn_v=(w_fvT, ffn_act, 0, ffn_v_made))
                channel_blocks = dict(q=(0, q_made), k=(1, k_made), ffn_k=(2, ffn_k_made))
                if n == 0:
                    pe.wait_ge(*spare_free(job, it))
                if what in token_blocks:
                    if n == 0:
                        if what == "o":
                            pe.wait_ge(*yT_stored.after(it, 1))
                        if what == "ffn_v":
                            pe.wait_ge(*ffn_k_taken.after(it if which == 0 else late, 1))
                        if what == "gate":
                            pe.wait_ge(*mixed.after(it, 1))
                        if what == "v":
                            pe.wait_ge(*xf_stored.after(it, 1))
                    weights, src, first, done = token_blocks[what]
                    t, ci = n // 2, n % 2
                    at = first + P * (2 * which + t)
                    last = nc.tensor.matmul(dst[:, E * t:E * (t + 1)], src[:, ci, at:at + P], weights[:, ci, :],
                                            start=(ci == 0), stop=(ci == CH - 1))
                    if n == 3:
                        last.then_inc(done.sem, 1)
                elif what in channel_blocks:
                    if n == 0:
                        pe.wait_ge(*(xk_rested if what == "ffn_k" else x_rested).after(it, 1))
                    w, done = channel_blocks[what]
                    ci, pair = n // 3, n % 3
                    weights = (w_high, w_high, w_low)[pair][w]
                    src = (x_high, x_low, x_high)[pair]
                    last = nc.tensor.matmul(dst[:, :], weights[:, ci, P * which:P * (which + 1)],
                                            src[:, ci, :], start=(n == 0), stop=(n == 3 * CH - 1))
                    if n == 3 * CH - 1:
                        last.then_inc(done.sem, 1)
                elif what == "heads":
                    pe.wait_ge(*o_taken.after(of, which + 2))
                    for t in range(TB):
                        last = nc.tensor.transpose(dst[:, P * t:P * (t + 1)], oT[:, P * t:P * (t + 1)], ident[:, :])
                    last.then_inc(heads_turned.sem, 1)
                elif what == "m":
                    pe.wait_ge(*m_rounded.after(of, which - 1))
                    nc.tensor.transpose(dst[0:HEADS, 0:P // 2].bitcast(F16),
                                        m16[which][:, :, :].rearrange("p h t -> p (h t)"),
                                        ident16[:, :]).then_inc(m_turned.sem, 1)
                elif what == "xf":
                    pe.wait_ge(*xn_made.after(late, 0))
                    for t in range(TB):
                        last = nc.tensor.transpose(dst[:, P * t:P * (t + 1)], xn[:, t, P * which:P * (which + 1)], ident[:, :])
                    last.then_inc(xn_turned.sem, 1)
                elif what == "yT":
                    pe.wait_ge(*y_made.after(late, 5))
                    for t in range(TB):
                        last = nc.tensor.transpose(dst[:, P * t:P * (t + 1)], y[:, t, P * which:P * (which + 1)], ident[:, :])
                    last.then_inc(y_turned.sem, 1)
                elif what == "pairs":
                    pe.wait_ge(*k_taken.after(it, 1))
                    for a in range(2):
                        for c in range(CH):
                            at = 32 * (2 * a + c)
                            last = nc.tensor.matmul(dst[at:at + 32, :], head_ones[:, :], band_prod[:, a, c, :],
                                                    start=True, stop=True, skip_group_check=True)
                    last.then_inc(pairs_summed.sem, 1)
                elif what == "band":
                    pe.wait_ge(*pairs_taken.after(it, 0))
                    for t in range(TB):
                        last = nc.tensor.transpose(dst[:, P * t:P * (t + 1)], pair_rows[:, P * t:P * (t + 1)], ident[:, :])
                    last.then_inc(band_turned.sem, 1)

            def body(it):
                for s in range(STEPS):
                    for k in range(SLOTS):
                        if it.is_first(-1):
                            wait_for_setup(8 * s + k)
                        at, pair = max_target(it, s)
                        if at.real(BATCHES):
                            g, i, qb = pair // 2, 2 * (pair % 2) + k // 4, TB - 1 - k % 4
                            if pair % 2 == 0 and k == 0:
                                pe.wait_ge(*stack_loaded[g].after(at if g == 3 else at - 1, 5))
                            pe.wait_ge(*max_taken.after(it, 8 * s + k - max_back(8 * s + k)))
                            nc.tensor.matmul(max_bank[MAX_BANK[8 * s + k]][:, 0:P * (qb + 1)], q_stack[g][:, i, P * qb:P * (qb + 1)],
                                             k_stack[g][:, i, 0:P * (qb + 1)], start=True,
                                             stop=True).then_inc(max_scored.sem, 1)
                        if k in FILL_SLOT and it.real(BATCHES):
                            f, g, i0 = FILL_SLOT[k], s // 2, 2 * (s % 2)
                            b, parts = (5 * s + f) % 2, FILLS[f]
                            if f == 0 and s % 2 == 0:
                                pe.wait_ge(*m_row[g].after(it - 1 if g == 0 else it, 0))
                            pe.wait_ge(*probs_made.after(it, 5 * s + f - 2))
                            for h, j, col in parts:
                                last = nc.tensor.matmul(fill_bank[b][:, col:col + SEQ - P * j],
                                                        k_stack[g][:, i0 + h, P * j:P * (j + 1)],
                                                        q_stack[g][:, i0 + h, P * j:SEQ], start=True, stop=True)
                            last.then_inc(scored.sem, 1)
                        at = it if s >= 2 else it - 1
                        if k in (2, 5) and at.real(BATCHES):
                            g = (s - 2) // 2 % NG
                            j = 2 * (s % 2) + (k - 2) // 3
                            if j < TB - 1:
                                pe.wait_ge(*probs_masked.after(at, 8 * g + (4, 5, 7)[j]))
                            if j == 0:
                                pe.wait_ge(*o_taken.after(at, g + 1))
                                if g == 0:
                                    pe.wait_ge(*v_taken.after(at - 1, 1))
                            for i in range(GROUP):
                                last = nc.tensor.matmul(o_bank[32 * i:32 * (i + 1), P * j:SEQ],
                                                        v0[at.parity][:, j, GROUP * g + i, :],
                                                        probs[g % 2][:, i, KEY_AT[j]:KEY_AT[j] + SEQ - P * j],
                                                        start=(j == 0), stop=(j == TB - 1), skip_group_check=True)
                            if j == TB - 1:
                                last.then_inc(o_added.sem, 1)
                        for job, (_, _, ahead, _, _, slots) in enumerate(JOBS):
                            if (it + ahead).real(BATCHES):
                                for part, slot in enumerate(slots):
                                    if slot == 8 * s + k:
                                        spare_work(it, job, part)

            iterations(pe, body)


_INS = ["L0_attn_x", "L0_attn_W_q", "L0_attn_b_q", "L0_attn_W_k", "L0_attn_b_k", "L0_attn_W_v", "L0_attn_b_v",
        "L0_attn_W_o", "L0_attn_b_o", "L0_attn_rel_k_table", "L0_attn_rel_v_table", "L0_ffn_W_r", "L0_ffn_W_k",
        "L0_ffn_W_v", "L0_ffn_mu_r", "L0_ffn_mu_k"]


def kernel(**inputs):
    import numpy as _np
    import concourse.bacc as _bacc
    from concourse import mybir as _mybir
    from concourse.bass_utils import run_bass_kernel_spmd as _run

    nc = _bacc.Bacc("TRN2", target_bir_lowering=False, num_devices=1, dynamic_dma_scratch_size=4096)
    arrays, args = {}, []
    for name in _INS:
        a = _np.ascontiguousarray(inputs[name])
        arrays[f"in_{name}_dram"] = a
        args.append(nc.dram_tensor(f"in_{name}_dram", a.shape, _mybir.dt.from_np(a.dtype), kind="ExternalInput").ap())
    shape = inputs["L0_attn_x"].shape
    args.append(nc.dram_tensor("out_0_dram", shape, _mybir.dt.float32, kind="ExternalOutput").ap())
    rwkv_attention_block(nc, *args)
    r = _run(nc, [arrays], core_ids=[0])
    return r.results[0]["out_0_dram"]
```
